# Optimizing a Trainium2 kernel written in Bass

```python
import numpy as np
import jax
import jax.numpy as jnp

def _softmax(x, axis=-1):
    return jax.nn.softmax(x, axis=axis)

def _gelu(x):
    return jax.nn.gelu(x, approximate=True)

def _silu(x):
    return jax.nn.silu(x)

def _sigmoid(x):
    return jax.nn.sigmoid(x)

def _layernorm(x, axis=-1, eps=1e-05):
    m = jnp.mean(x, axis=axis, keepdims=True)
    v = jnp.var(x, axis=axis, keepdims=True)
    return (x - m) / jnp.sqrt(v + eps)

def _scatter_add(tgt, idx, src, axis=0):
    return tgt.at[idx].add(src)

def _segment_sum(src, seg, n):
    return jax.ops.segment_sum(src, seg, n)
kernel_name = 'mk_seq_postln_d1_jaxref_r8_8279a6'

def setup_inputs(seed: int=0):
    np.random.seed(seed)
    _w = jnp.asarray

    def _L0_attn_setup():
        import jax, jax.numpy as jnp
        import numpy as np
        HIDDEN = 256
        N_HEADS = 32
        HEAD_DIM = HIDDEN // N_HEADS
        SEQ = 256
        BATCH = 1
        CHUNK = 32
        TOPK = 4
        THETA = 10000.0
        EPS = 1e-06
        NEG = jnp.float32(-1e+30)

        def _rope(t):
            D = t.shape[-1]
            pos = jnp.arange(t.shape[1], dtype=jnp.float32)
            inv_freq = 1.0 / THETA ** (jnp.arange(0, D, 2, dtype=jnp.float32) / D)
            freqs = pos[:, None] * inv_freq[None, :]
            cos = jnp.cos(freqs)[None, :, None, :]
            sin = jnp.sin(freqs)[None, :, None, :]
            t1, t2 = (t[..., :D // 2], t[..., D // 2:])
            return jnp.concatenate([t1 * cos - t2 * sin, t1 * sin + t2 * cos], axis=-1)
        key = jax.random.key(seed)
        ks = jax.random.split(key, 8)
        s = 0.02
        return {'hidden_states': jax.random.normal(ks[0], (BATCH, SEQ, HIDDEN), jnp.float32), 'Wq': jax.random.normal(ks[1], (HIDDEN, HIDDEN), jnp.float32) * s, 'Wk': jax.random.normal(ks[2], (HIDDEN, HIDDEN), jnp.float32) * s, 'Wv': jax.random.normal(ks[3], (HIDDEN, HIDDEN), jnp.float32) * s, 'Wo': jax.random.normal(ks[4], (HIDDEN, HIDDEN), jnp.float32) * s, 'Wg1': jax.random.normal(ks[5], (HEAD_DIM, HIDDEN), jnp.float32) * s, 'Wg2': jax.random.normal(ks[6], (HIDDEN, HEAD_DIM), jnp.float32) * s, 'o_norm_weight': jnp.ones((HEAD_DIM,), jnp.float32)}
    _L0_attn_in = _L0_attn_setup()

    def _L0_ffn_setup():
        import jax, jax.numpy as jnp
        import numpy as np
        D_MODEL, D_FF, NS, NR, KR = (256, 176, 2, 16, 4)
        B, S = (4, 256)

        def _moe_forward(u, shared_w1, shared_b1, shared_w2, shared_b2, routed_w1, routed_b1, routed_w2, routed_b2, centroids, bias):
            b, s, d = u.shape
            flat = u.reshape(-1, d)
            T = flat.shape[0]
            h = jax.nn.relu(jnp.einsum('td,ndf->ntf', flat, shared_w1) + shared_b1[:, None, :])
            shared_out = jnp.einsum('ntf,nfd->td', h, shared_w2) + shared_b2.sum(0)
            out = flat + shared_out
            scores = jax.nn.sigmoid(flat @ centroids.T) + bias
            vals, idx = jax.lax.top_k(scores, KR)
            gating = jnp.zeros_like(scores).at[jnp.arange(T)[:, None], idx].set(vals)
            gating = gating / jnp.clip(gating.sum(-1, keepdims=True), 1e-08)

            def step(acc, ew):
                w1, b1, w2, b2, g = ew
                hj = jax.nn.relu(flat @ w1 + b1)
                yj = hj @ w2 + b2
                return (acc + yj * g[:, None], None)
            rout0 = jnp.zeros_like(flat)
            rout, _ = jax.lax.scan(step, rout0, (routed_w1, routed_b1, routed_w2, routed_b2, gating.T))
            return (out + rout).reshape(b, s, d)
        key = jax.random.key(seed)
        ks = jax.random.split(key, 10)
        s1 = 1.0 / np.sqrt(D_MODEL)
        s2 = 1.0 / np.sqrt(D_FF)
        return {'u': jax.random.normal(ks[0], (B, S, D_MODEL), dtype=jnp.float32), 'shared_w1': jax.random.normal(ks[1], (NS, D_MODEL, D_FF), dtype=jnp.float32) * s1, 'shared_b1': jnp.zeros((NS, D_FF), dtype=jnp.float32), 'shared_w2': jax.random.normal(ks[2], (NS, D_FF, D_MODEL), dtype=jnp.float32) * s2, 'shared_b2': jnp.zeros((NS, D_MODEL), dtype=jnp.float32), 'routed_w1': jax.random.normal(ks[3], (NR, D_MODEL, D_FF), dtype=jnp.float32) * s1, 'routed_b1': jnp.zeros((NR, D_FF), dtype=jnp.float32), 'routed_w2': jax.random.normal(ks[4], (NR, D_FF, D_MODEL), dtype=jnp.float32) * s2, 'routed_b2': jnp.zeros((NR, D_MODEL), dtype=jnp.float32), 'centroids': jax.random.normal(ks[5], (NR, D_MODEL), dtype=jnp.float32) * s1, 'bias': jnp.zeros((NR,), dtype=jnp.float32)}
    _L0_ffn_in = _L0_ffn_setup()
    _d = {'L0_attn_hidden_states': _L0_attn_in['hidden_states'], 'L0_attn_Wq': _L0_attn_in['Wq'], 'L0_attn_Wk': _L0_attn_in['Wk'], 'L0_attn_Wv': _L0_attn_in['Wv'], 'L0_attn_Wo': _L0_attn_in['Wo'], 'L0_attn_Wg1': _L0_attn_in['Wg1'], 'L0_attn_Wg2': _L0_attn_in['Wg2'], 'L0_attn_o_norm_weight': _L0_attn_in['o_norm_weight'], 'L0_ffn_shared_w1': _L0_ffn_in['shared_w1'], 'L0_ffn_shared_b1': _L0_ffn_in['shared_b1'], 'L0_ffn_shared_w2': _L0_ffn_in['shared_w2'], 'L0_ffn_shared_b2': _L0_ffn_in['shared_b2'], 'L0_ffn_routed_w1': _L0_ffn_in['routed_w1'], 'L0_ffn_routed_b1': _L0_ffn_in['routed_b1'], 'L0_ffn_routed_w2': _L0_ffn_in['routed_w2'], 'L0_ffn_routed_b2': _L0_ffn_in['routed_b2'], 'L0_ffn_centroids': _L0_ffn_in['centroids'], 'L0_ffn_bias': _L0_ffn_in['bias']}
    _x0 = _d['L0_attn_hidden_states']
    _d['L0_attn_hidden_states'] = jax.random.normal(jax.random.fold_in(jax.random.key(seed), 1), (8, 512, 256), dtype=_x0.dtype)
    del _x0
    return _d

def reference(L0_attn_hidden_states, L0_attn_Wq, L0_attn_Wk, L0_attn_Wv, L0_attn_Wo, L0_attn_Wg1, L0_attn_Wg2, L0_attn_o_norm_weight, L0_ffn_shared_w1, L0_ffn_shared_b1, L0_ffn_shared_w2, L0_ffn_shared_b2, L0_ffn_routed_w1, L0_ffn_routed_b1, L0_ffn_routed_w2, L0_ffn_routed_b2, L0_ffn_centroids, L0_ffn_bias):

    def _L0_attn_ref(hidden_states, Wq, Wk, Wv, Wo, Wg1, Wg2, o_norm_weight):
        import jax, jax.numpy as jnp
        import numpy as np
        HIDDEN = 256
        N_HEADS = 32
        HEAD_DIM = HIDDEN // N_HEADS
        SEQ = 256
        BATCH = 1
        CHUNK = 32
        TOPK = 4
        THETA = 10000.0
        EPS = 1e-06
        NEG = jnp.float32(-1e+30)

        def _rope(t):
            D = t.shape[-1]
            pos = jnp.arange(t.shape[1], dtype=jnp.float32)
            inv_freq = 1.0 / THETA ** (jnp.arange(0, D, 2, dtype=jnp.float32) / D)
            freqs = pos[:, None] * inv_freq[None, :]
            cos = jnp.cos(freqs)[None, :, None, :]
            sin = jnp.sin(freqs)[None, :, None, :]
            t1, t2 = (t[..., :D // 2], t[..., D // 2:])
            return jnp.concatenate([t1 * cos - t2 * sin, t1 * sin + t2 * cos], axis=-1)
        B, S, _ = hidden_states.shape
        H, D, C = (N_HEADS, HEAD_DIM, CHUNK)
        NC = S // C
        q = (hidden_states @ Wq.T).reshape(B, S, H, D)
        k = (hidden_states @ Wk.T).reshape(B, S, H, D)
        v = (hidden_states @ Wv.T).reshape(B, S, H, D)
        q, k = (_rope(q), _rope(k))
        kmean = k.reshape(B, NC, C, H, D).mean(axis=2)
        gate = jnp.einsum('bshd,bnhd->bhsn', q, kmean)
        pos = jnp.arange(S)
        q_chunk = pos // C
        chunk_ids = jnp.arange(NC)
        future = chunk_ids[None, :] > q_chunk[:, None]
        self_blk = chunk_ids[None, :] == q_chunk[:, None]
        gate = jnp.where(future[None, None], NEG, gate)
        gate = jnp.where(self_blk[None, None], -NEG, gate)
        _, topk_idx = jax.lax.top_k(gate, TOPK)
        sel = jax.nn.one_hot(topk_idx, NC, dtype=jnp.bool_).any(axis=-2)
        allowed = jnp.take(sel, q_chunk, axis=-1)
        causal = pos[None, :] <= pos[:, None]
        allowed = allowed & causal[None, None]
        scale = 1.0 / np.sqrt(D)
        scores = jnp.einsum('bshd,bthd->bhst', q, k) * scale
        scores = jnp.where(allowed, scores, NEG)
        p = jax.nn.softmax(scores, axis=-1)
        o = jnp.einsum('bhst,bthd->bshd', p, v)
        g = (hidden_states @ Wg1.T @ Wg2.T).reshape(B, S, H, D)
        rms = jax.lax.rsqrt(jnp.mean(o * o, axis=-1, keepdims=True) + EPS)
        o = o * rms * o_norm_weight * jax.nn.sigmoid(g)
        return o.reshape(B, S, H * D) @ Wo.T

    def _L0_ffn_ref(u, shared_w1, shared_b1, shared_w2, shared_b2, routed_w1, routed_b1, routed_w2, routed_b2, centroids, bias):
        import jax, jax.numpy as jnp
        import numpy as np
        D_MODEL, D_FF, NS, NR, KR = (256, 176, 2, 16, 4)
        B, S = (4, 256)

        def _moe_forward(u, shared_w1, shared_b1, shared_w2, shared_b2, routed_w1, routed_b1, routed_w2, routed_b2, centroids, bias):
            b, s, d = u.shape
            flat = u.reshape(-1, d)
            T = flat.shape[0]
            h = jax.nn.relu(jnp.einsum('td,ndf->ntf', flat, shared_w1) + shared_b1[:, None, :])
            shared_out = jnp.einsum('ntf,nfd->td', h, shared_w2) + shared_b2.sum(0)
            out = flat + shared_out
            scores = jax.nn.sigmoid(flat @ centroids.T) + bias
            vals, idx = jax.lax.top_k(scores, KR)
            gating = jnp.zeros_like(scores).at[jnp.arange(T)[:, None], idx].set(vals)
            gating = gating / jnp.clip(gating.sum(-1, keepdims=True), 1e-08)

            def step(acc, ew):
                w1, b1, w2, b2, g = ew
                hj = jax.nn.relu(flat @ w1 + b1)
                yj = hj @ w2 + b2
                return (acc + yj * g[:, None], None)
            rout0 = jnp.zeros_like(flat)
            rout, _ = jax.lax.scan(step, rout0, (routed_w1, routed_b1, routed_w2, routed_b2, gating.T))
            return (out + rout).reshape(b, s, d)
        return _moe_forward(u, shared_w1, shared_b1, shared_w2, shared_b2, routed_w1, routed_b1, routed_w2, routed_b2, centroids, bias)
    x = L0_attn_hidden_states
    x = _layernorm(x + _L0_attn_ref(x, L0_attn_Wq, L0_attn_Wk, L0_attn_Wv, L0_attn_Wo, L0_attn_Wg1, L0_attn_Wg2, L0_attn_o_norm_weight), axis=-1)
    x = _layernorm(x + _L0_ffn_ref(x, L0_ffn_shared_w1, L0_ffn_shared_b1, L0_ffn_shared_w2, L0_ffn_shared_b2, L0_ffn_routed_w1, L0_ffn_routed_b1, L0_ffn_routed_w2, L0_ffn_routed_b2, L0_ffn_centroids, L0_ffn_bias), axis=-1)
    return x

_drawn_inputs = setup_inputs


def setup_inputs(seed=0):
    import zlib

    import numpy as np

    out = dict(_drawn_inputs(seed))
    spreads = {'L0_attn_o_norm_weight': (1.0, 0.2),
     'L0_ffn_shared_b1': (0.0, 0.1),
     'L0_ffn_shared_b2': (0.0, 0.1),
     'L0_ffn_routed_b1': (0.0, 0.54),
     'L0_ffn_routed_b2': (0.0, 0.368),
     'L0_ffn_bias': (0.0, 0.1)}
    factors = {'L0_attn_Wg1': 8.0, 'L0_attn_Wg2': 8.0}
    for name, (base, spread) in spreads.items():
        noise = np.random.default_rng([zlib.crc32(name.encode()), seed]).standard_normal(out[name].shape)
        drawn = base * np.exp(spread * noise) if base else spread * noise
        out[name] = jnp.asarray(drawn.astype(out[name].dtype))
    for name, factor in factors.items():
        out[name] = (out[name] * factor).astype(out[name].dtype)
    return out
```

```python
from contextlib import ExitStack

import concourse.bass as bass
from concourse import mybir
from concourse.alu_op_type import AluOpType as ALU

ACT = mybir.ActivationFunctionType
AX = mybir.AxisListType
F32 = mybir.dt.float32
F16 = mybir.dt.float16
BF16 = mybir.dt.bfloat16
I32 = mybir.dt.int32

P = 128
B, S, D = 8, 512, 256
H, HD = 32, 8
CHUNK, TOPK = 32, 4
NCH = S // CHUNK
NT = S // P
KT = D // P
CPT = P // CHUNK
HG = 4
NG = H // HG
SLOTS = 4
HW = 64
CR = SLOTS * HD
QW = D + D + D + HD
NE, NS, DF, KR = 16, 2, 176, 4
FS, FR = NS * DF, NE * DF
NSH = 3
CHUNKS = [(0, P), (P, P), (2 * P, FS - 2 * P)] + [(FS + P * i, P) for i in range(FR // P)]
NC = len(CHUNKS)
SCALE = HD ** -0.5
BIG = 1e30
PAD = -3e38
CHOSEN = 3e38
TOPW = NCH + 5
UNIT = 2.0 ** 15
OFF = 2.0 ** 15
ROOT = 0x5F3759DF
MOFF = {3: 0, 2: 512, 0: 896, 1: 1024}
POFF = {0: 0, 1: 512, 3: 896, 2: 1024}
SW = 1280
NU = 20
RING = 4
C_FIRST, C_TOPK, C_MAX, C_BIAS, C_OUT = (0, 3), (3, 11), (11, 19), (19, 22), (22, 25)

C_ID, C_COS, C_SIN, C_AVG, C_BM, C_GM, C_SM, C_ONW, C_RB, C_B1 = 0, 128, 144, 160, 164, 180, 244, 308, 309, 325
C_W = C_B1 + NC
H_ID, H_IND, H_W = 0, 128, 192
G_ID, G_CQ, G_CK, G_W = 0, 128, 256, 384
ROW_G1, ROW_GT = 32, 64


def build(nc, xT_d, x_d, wa_d, wg2_d, wo_d, w1_d, w2_d, cent_d, b2_d, cf_d, ch_d, cg_d, one_d, out_d):
    with ExitStack() as ctx:
        def sb(name, shape, dt=F32):
            return ctx.enter_context(nc.sbuf_tensor(name, shape, dt))

        def sem(name):
            return ctx.enter_context(nc.semaphore(name))

        W1 = sb("W1", [P, 2, KT, FS + FR], F16)
        W2 = sb("W2", [P, 2, NC, D], F16)
        WA = sb("WA", [P, KT, QW])
        WO = sb("WO", [P, KT, D])
        CENT = sb("CENT", [P, 2, KT, NE], F16)
        ROWS = sb("ROWS", [P, FR], F16)
        B2 = ROWS[ROW_GT:ROW_GT + NE + NS, 0:2 * D].bitcast(F32)
        WG2 = ROWS[ROW_G1:ROW_G1 + HD, 0:2 * D].bitcast(F32)
        onehot = ROWS[0:2 * NE, :]
        CF = sb("CF", [P, C_W])
        CH = sb("CH", [P, H_W], F16)
        CG = sb("CG", [P, G_W], BF16)
        xT = sb("xT", [P, KT, S])
        x = xT[:, :, :].rearrange("p k s -> p (k s)").rearrange("p (t d) -> p t d", t=NT)
        UK = sb("UK", [P, 6144])
        UQ = sb("UQ", [P, HG * SW])
        EK = UK[:, 0:4096].bitcast(F16).rearrange("p (t h w) -> p t h w", t=NT, h=H)
        rot = UK[:, 4096:6144].rearrange("p (t c) -> p t c", t=NT)
        EQ = UQ[:, 0:4096].bitcast(F16).rearrange("p (t h w) -> p t h w", t=NT, h=H)
        PT = (UK[:, 0:HG * SW].rearrange("p (h w) -> p h w", h=HG),
              UQ[:, :].rearrange("p (h w) -> p h w", h=HG))
        ropeb = sb("ropeb", [P, 2 * D])
        KB = ropeb[:, :].rearrange("p (k d) -> p k d", k=KT)
        osb = ropeb
        v = sb("v", [P, NT, D])
        qT = sb("qT", [P, KT, S])
        eg = qT[:, :, :].rearrange("p k s -> p (k s)").rearrange("p (t d) -> p t d", t=NT)
        gmask = sb("gmask", [P, H, TOPW])
        rep = sb("rep", [P, H, TOPW])
        cbias = sb("cbias", [P, NT, H, NCH], F16)
        qET = sb("qET", [P, H // 2, S], F16)
        qf = qET[:, :, :].rearrange("p a s -> p (a s)").bitcast(F32)
        aT = qf[:, 0:1024].rearrange("p (k s) -> p k s", k=KT)
        yout = qf[:, 1024:2048].rearrange("p (t d) -> p t d", t=NT)
        sq = qf[:, 2048:3072].rearrange("p (h d) -> p h d", d=HD)
        kz = (sb("kz0", [P, H // 2, S], F16),
              sb("kz1", [P, H // 2, S], F16))
        CM = sb("CM", [P, H, SW // CHUNK])
        cmf = CM[:, :, :].rearrange("p h c -> p (h c)")
        top8 = cmf[:, 0:H * 8].rearrange("p (h e) -> p h e", h=H)
        otok = cmf[:, 0:NT * H * (HD + 1)].rearrange("p (h d) -> p h d", d=HD + 1)
        negm = sb("negm", [P, H])
        vst = sb("vst", [P, NT, HG, 32])
        ms = sb("ms", [P, NT * H])
        ry = sb("ry", [P, NT * H])
        rt = sb("rt", [P, NT * H])
        st6 = sb("st6", [P, NT, 6])
        mv = sb("mv", [P, NT, 2])
        x1n = sb("x1n", [P, NT, D])
        x1T = sb("x1T", [P, 2, KT, S], F16)
        er = sb("er", [P, NT, NE])
        CENTF = er[:, 0:KT, :]
        sc = sb("sc", [P, NT, TOPW])
        rtop = sb("rtop", [P, NT, 8])
        rrep = sb("rrep", [P, NT, TOPW])
        gat = sb("gat", [P, NT, NE])
        gsum = sb("gsum", [P, NT])
        gext = sb("gext", [P, NT, NE + NS])
        gsp = sb("gsp", [P, NT, 2, NE], F16)
        GR = sb("GR", [P, S])
        gT = GR[ROW_GT:ROW_GT + NE + NS, :]
        g1T = GR[ROW_G1:ROW_G1 + HD, :]
        gTp = GR[0:2 * NE, 0:S // 2].bitcast(F16)
        hr = sb("hr", [P, S])
        hp = sb("hp", [P, 2, 2, S], F16)

        PS = ctx.enter_context(nc.psum_tensor("PS", [P, 8, 512], F32))
        PSH = PS[:, :, :].bitcast(F16)
        BK_H, BK_G, BK_Y = 4, 5, 6
        BK_PV, BK_OT = 4, 5

        ident = CF[:, C_ID:C_ID + P]
        cos = CF[:, C_COS:C_COS + 16].rearrange("p (t f) -> p t f", t=NT)
        sin = CF[:, C_SIN:C_SIN + 16].rearrange("p (t f) -> p t f", t=NT)
        avg = CF[:, C_AVG:C_AVG + CPT]
        bmask = CF[:, C_BM:C_BM + 16]
        gm_c = CF[:, C_GM:C_GM + 64].rearrange("p (t n) -> p t n", t=NT)
        sm_c = CF[:, C_SM:C_SM + 64].rearrange("p (t n) -> p t n", t=NT)
        onw = CF[:, C_ONW:C_ONW + 1]
        rbias = CF[:, C_RB:C_RB + NE]
        b1 = CF[:, C_B1:C_B1 + NC]
        identh = CH[:, H_ID:H_ID + P]
        ind = CH[:, H_IND:H_IND + 64].rearrange("p (t n) -> p t n", t=NT)
        identb = CG[:, G_ID:G_ID + P]
        causal_q = CG[:, G_CQ:G_CQ + P]
        causal_k = CG[:, G_CK:G_CK + P]

        s_const = sem("s_const")
        s_w = sem("s_w")
        s_init = sem("s_init")
        s_one = sem("s_one")
        act_w = sem("act_w")
        dve_w = sem("dve_w")
        s_xT = sem("s_xT")
        s_x = sem("s_x")
        s_out = sem("s_out")
        pe_proj = sem("pe_proj")
        dve_rope = sem("dve_rope")
        act_v = sem("act_v")
        act_e = sem("act_e")
        pool_e = sem("pool_e")
        pe_qT = sem("pe_qT")
        act_qT = sem("act_qT")
        pe_km = sem("pe_km")
        dve_kb = sem("dve_kb")
        pe_gate = sem("pe_gate")
        dve_gm = sem("dve_gm")
        pe_ek = sem("pe_ek")
        act_kz = sem("act_kz")
        pe_eq = sem("pe_eq")
        act_eq = sem("act_eq")
        pe_mx = sem("pe_mx")
        dve_cm = sem("dve_cm")
        dve_bias = sem("dve_bias")
        pe_eq2 = sem("pe_eq2")
        act_eq2 = sem("act_eq2")
        pe_g1 = sem("pe_g1")
        act_g1 = sem("act_g1")
        pe_g = sem("pe_g")
        act_eg = sem("act_eg")
        pe_sc = sem("pe_sc")
        act_p = sem("act_p")
        pool_v = sem("pool_v")
        pe_pv = sem("pe_pv")
        dve_o = sem("dve_o")
        pe_oT = sem("pe_oT")
        dve_otok = sem("dve_otok")
        dve_on = sem("dve_on")
        pe_aT = sem("pe_aT")
        act_aT = sem("act_aT")
        pe_att = sem("pe_att")
        dve_x1 = sem("dve_x1")
        dve_ln = sem("dve_ln")
        pe_x1T = sem("pe_x1T")
        act_x1T = sem("act_x1T")
        dve_x1T = sem("dve_x1T")
        pe_rt = sem("pe_rt")
        act_rt = sem("act_rt")
        dve_g = sem("dve_g")
        pe_gT = sem("pe_gT")
        act_gT = sem("act_gT")
        pe_h = sem("pe_h")
        act_h = sem("act_h")
        dve_h = sem("dve_h")
        act_hp = sem("act_hp")
        pool_hp = sem("pool_hp")
        pe_y = sem("pe_y")
        dve_z = sem("dve_z")
        dve_out = sem("dve_out")

        def settled_wait(eng, which, count):
            if not isinstance(count, int):
                count = eng.to_reg(count)
                eng.wait_ge(s_one, 1)
            eng.wait_ge(which, count)

        def max_blocks(u):
            return (((0, 3),), ((0, 2), (0, 0)), ((0, 1), (1, 1)), ((1, 3),), ((1, 2), (1, 0)))[u]

        def prob_blocks(u):
            return (((0, 0),), ((0, 1), (0, 3)), ((0, 2), (1, 2)), ((1, 0),), ((1, 1), (1, 3)))[u]

        block = ctx.enter_context(nc.Block())
        NCONST = 10

        @block.sync
        def _(sp):
            sp.sem_inc(s_out, 16)
            for dst, src in ((CF[:, :], cf_d), (CH[:, :], ch_d), (CG[:, :], cg_d),
                             (WA[:, :, :], wa_d.rearrange("(k p) n -> p k n", p=P)),
                             (WG2, wg2_d), (B2, b2_d), (onehot, one_d),
                             (WO[:, :, :], wo_d.rearrange("(k p) n -> p k n", p=P)),
                             (CENTF[:, :, :], cent_d.rearrange("(k p) n -> p k n", p=P))):
                sp.dma_start(dst, src).then_inc(s_const, 16)
            w1_v = w1_d.rearrange("(k p) n -> k p n", p=P)
            w2_v = w2_d.rearrange("(c p) n -> p c n", p=P)
            sp.dma_start(UK[:, 0:FS + FR], w1_v[0]).then_inc(s_w, 16)
            sp.wait_ge(s_w, 16)
            sp.dma_start(UQ[:, 0:FS + FR], w1_v[1]).then_inc(s_w, 16)
            sp.wait_ge(s_w, 32)
            sp.dma_start(qf[:, 0:13 * D].rearrange("p (c n) -> p c n", n=D), w2_v[:, 0:13]).then_inc(s_w, 16)
            sp.wait_ge(s_w, 48)
            k0f = kz[0][:, :, :].rearrange("p a s -> p (a s)").bitcast(F32)
            sp.dma_start(k0f[:, 0:12 * D].rearrange("p (c n) -> p c n", n=D), w2_v[:, 13:NC]).then_inc(s_w, 16)

            def load_xT(b):
                settled_wait(sp, dve_x1, b * 2 + 1)
                sp.dma_start(xT[:, :, :], xT_d[bass.ds(b, 1)].rearrange("o (k p) s -> p (o k) s", p=P)).then_inc(s_xT, 16)

            def load_x(b):
                settled_wait(sp, pe_g1, b + 1)
                sp.dma_start(x, x_d[bass.ds(b, 1)].rearrange("o (t p) d -> p (o t) d", p=P)).then_inc(s_x, 16)

            def store(b):
                settled_wait(sp, dve_out, (b + 1) * NT)
                sp.dma_start(out_d[bass.ds(b, 1)].rearrange("o (t p) d -> p (o t) d", p=P), yout).then_inc(s_out, 16)

            load_xT(0)
            load_x(0)
            with sp.Fori(1, B) as b:
                load_xT(b)
                load_x(b)
                store(b - 1)
            store(B - 1)
            sp.wait_ge(s_out, 16 * B + 16)

        @block.tensor
        def _(pe):
            for credit in (pe_eq2, pe_km, pe_gate, pe_mx, pe_oT):
                pe.sem_inc(credit, 1)
            pe.sem_inc(pe_y, 2)
            pe.sem_inc(pe_pv, 2)
            pe.wait_ge(s_const, 16 * (NCONST - 1))
            pe.wait_ge(s_init, 3)
            pe.wait_ge(act_w, 5)
            pe.wait_ge(dve_w, 6)

            def project(b):
                pe.wait_ge(s_xT, 16 * b + 16)
                pe.wait_ge(dve_x1, 2 * b + 1)
                for j in range(NT):
                    if j >= 2:
                        pe.wait_ge(dve_rope, b * NT + j - 1)
                        pe.wait_ge(act_v, b * NT + j - 1)
                    for k in range(KT):
                        pe.matmul(PS[:, j % 2, :], xT[:, k, j * P:(j + 1) * P], WA[:, k, 0:2 * D],
                                  start=(k == 0), stop=(k == KT - 1))
                    for k in range(KT):
                        mm = pe.matmul(PS[:, 2 + j % 2, 0:D], xT[:, k, j * P:(j + 1) * P], WA[:, k, 2 * D:3 * D],
                                       start=(k == 0), stop=(k == KT - 1))
                    mm.then_inc(pe_proj, 1)

            def chunk_gates(b):
                pe.wait_ge(dve_rope, (b + 1) * NT)
                pe.wait_ge(act_v, (b + 1) * NT)
                for m in range(KT):
                    for j in range(NT):
                        mm = pe.transpose(PS[:, m, j * P:(j + 1) * P], rot[:, j, m * P:(m + 1) * P], ident)
                    mm.then_inc(pe_qT, 1)
                for m in range(KT):
                    for j in range(NT):
                        mm = pe.matmul(PS[:, 2, m * NCH + j * CPT:m * NCH + (j + 1) * CPT],
                                       rot[:, j, D + m * P:D + (m + 1) * P], avg, start=True, stop=True)
                mm.then_inc(pe_km, 1)
                pe.wait_ge(act_qT, (b + 1) * KT)
                pe.wait_ge(dve_kb, (b + 1) * KT)
                for j, bank in ((1, 3), (2, 0), (3, 1)):
                    for m in range(KT):
                        mm = pe.matmul(PS[:, bank, m * D:(m + 1) * D], qT[:, m, j * P:(j + 1) * P], KB[:, m, :],
                                       start=True, stop=True)
                    mm.then_inc(pe_gate, 1)

            def stack(E, bank, g, done):
                for j in range(NT):
                    for pr in range(2):
                        mm = pe.transpose(PSH[:, bank, pr * S + j * P:pr * S + (j + 1) * P],
                                          E[:, j, bass.ds(g * HG + 2 * pr, 2), :].rearrange("p h w -> p (h w)"), identh)
                mm.then_inc(done, 1)

            def score_unit(g8, u, by_key):
                pair = g8 * 4 + u // 5
                blocks = (prob_blocks if by_key else max_blocks)(u % 5)
                for n, (hh, t) in enumerate(blocks):
                    if by_key:
                        w = S - P * t
                        o = POFF[t] % 512 if t != 2 else 256 * hh
                        lhsT, rhs, diag = kz[hh][:, bass.ds(pair, 1), t * P:(t + 1) * P], qET[:, bass.ds(pair, 1), t * P:S], o
                    else:
                        w = P * (t + 1)
                        o = MOFF[t] % 512 if t != 1 else 256 * hh
                        lhsT, rhs, diag = qET[:, bass.ds(pair, 1), t * P:(t + 1) * P], kz[hh][:, bass.ds(pair, 1), 0:w], o + w - P
                    pe.matmul(PS[:, u % RING, o:o + w], lhsT.rearrange("p o s -> p (o s)"), rhs.rearrange("p o s -> p (o s)"),
                              start=True, stop=False)
                    mm = pe.matmul(PS[:, u % RING, diag:diag + P], identb, causal_k if by_key else causal_q,
                                   start=False, stop=True)
                mm.then_inc(pe_sc if by_key else pe_mx, 1)

            def x1_transpose(m):
                pe.wait_ge(dve_ln, (m + 1) * NT)
                for k in range(KT):
                    for j in range(NT):
                        mm = pe.transpose(PS[:, 4 + k, j * P:(j + 1) * P], x1n[:, j, k * P:(k + 1) * P], ident)
                    mm.then_inc(pe_x1T, 1)

            def router(m):
                pe.wait_ge(dve_z, 2 * m + 1)
                pe.wait_ge(act_x1T, (m + 1) * KT)
                pe.wait_ge(dve_x1T, (m + 1) * KT)
                for j in range(NT):
                    for n, (k, a, c) in enumerate((k, a, c) for k in range(KT) for a, c in ((0, 0), (0, 1), (1, 0))):
                        mm = pe.matmul(PS[:, BK_Y, j * NE:(j + 1) * NE], x1T[:, a, k, j * P:(j + 1) * P], CENT[:, c, k, :],
                                       start=(n == 0), stop=(n == 3 * KT - 1))
                mm.then_inc(pe_rt, 1)

            def gate_rows(m):
                settled_wait(pe, dve_g, m + 1)
                for j in range(NT):
                    pe.transpose(PSH[0:2 * NE, BK_Y + 1, j * P:(j + 1) * P], gsp[:, j].rearrange("p a e -> p (a e)"), identh)
                for j in range(NT):
                    mm = pe.matmul(PS[ROW_GT:ROW_GT + NE + NS, BK_Y, j * P:(j + 1) * P], gext[:, j, :], ident, start=True, stop=True,
                                   tile_position=(0, ROW_GT))
                mm.then_inc(pe_gT, 1)

            def open_outputs(m):
                pe.wait_ge(act_gT, 2 * m + 2)
                for j in range(NT):
                    pe.matmul(PS[:, BK_Y + j // 2, (j % 2) * D:(j % 2 + 1) * D], gT[:, j * P:(j + 1) * P], B2,
                              start=(j % 2 == 0), stop=False, skip_group_check=True, tile_position=(ROW_GT, 0))

            def hidden_cols(c):
                return CHUNKS[c] if isinstance(c, int) else (FS + (c - NSH) * P, P)

            def up(m, c, part):
                f0, w = hidden_cols(c)
                if part == 0:
                    pe.wait_ge(act_h, m * NC + c + 1)
                for n in (2 * part, 2 * part + 1):
                    k, (a, e) = n // 3, ((0, 0), (0, 1), (1, 0))[n % 3]
                    mm = pe.matmul(PS[0:w, BK_H, :], W1[:, a, k, bass.ds(f0, w)], x1T[:, e, k, :],
                                   start=(n == 0), stop=(n == 5))
                if part == 2 and isinstance(c, int) and c < NSH:
                    mm.then_inc(pe_h, 1)

            def gate_of(m, c):
                pe.wait_ge(dve_h, m * (NC - NSH) + c - NSH + 1)
                pe.matmul(PS[:, BK_G, :], onehot[:, bass.ds((c - NSH) * P, P)], gTp, start=True, stop=True).then_inc(pe_h, 1)

            def down(m, c, j):
                w = CHUNKS[c][1] if isinstance(c, int) else P
                if j == 0:
                    pe.wait_ge(pool_hp, m * NC + c + 2)
                cc = c if isinstance(c, int) else c
                for a, e in ((0, 0), (0, 1), (1, 0)):
                    last = isinstance(c, int) and c == NC - 1 and (a, e) == (1, 0)
                    slot = c % 2 if isinstance(c, int) else None
                    mm = pe.matmul(PS[:, BK_Y + j // 2, (j % 2) * D:(j % 2 + 1) * D],
                                   hp[0:w, slot, a, j * P:(j + 1) * P],
                                   W2[0:w, e, cc, :], start=False, stop=last, skip_group_check=True)
                if j == NT - 1:
                    mm.then_inc(pe_y, 1)

            def chunk_run(m, first, last, lag):
                for c in range(first, last):
                    for part in range(3):
                        up(m, c, part)
                    if c >= NSH:
                        gate_of(m, c)
                    if c > 0:
                        for j in range(NT):
                            down(m, c - 1, j)

            def turn(b, m):
                if m is not None:
                    x1_transpose(m)
                project(b)
                if m is not None:
                    router(m)
                chunk_gates(b)
                if m is not None:
                    for part in range(3):
                        up(m, 0, part)
                    gate_rows(m)
                    open_outputs(m)
                    chunk_run(m, 1, C_FIRST[1], 1)
                pe.wait_ge(dve_kb, (b + 1) * KT)
                settled_wait(pe, dve_gm, b * 3 + 1)
                with pe.Fori(0, NG // 2) as i:
                    for u in range(2):
                        n = b * NG + i * 2 + u
                        if m is not None:
                            c = Routed(i * 2 + C_TOPK[0] + u, u + C_TOPK[0])
                            for part in range(3):
                                up_r(m, c, part)
                            gate_of(m, c.value)
                            for j in range(NT):
                                down_r(m, c.before(), j)
                        if u == 0:
                            pe.wait_ge(pool_e, (b + 1) * NT + 1)
                        pe.wait_ge(act_kz, 2 * n + 1)
                        stack(EK, 2, i * 2 + u, pe_ek)
                        pe.wait_ge(act_eq, n + 1)
                        stack(EQ, 3, i * 2 + u, pe_eq)
                pe.wait_ge(act_kz, (b + 1) * 2 * NG + 1)
                pe.wait_ge(act_eq, (b + 1) * NG + 1)
                settled_wait(pe, dve_gm, (b + 1) * 3)
                with pe.Fori(0, NG // 2) as i:
                    for u in range(NU):
                        pe.wait_ge(dve_cm, b * 4 * NU + i * NU + u + 1)
                        score_unit(i, u, False)
                        half, s = divmod(u, NU // 2)
                        if m is not None:
                            c = Routed(i * 2 + C_MAX[0] + half, half + C_MAX[0])
                            if s < 3:
                                up_r(m, c, s)
                            elif s == 3:
                                gate_of(m, c.value)
                            elif s < 4 + NT:
                                down_r(m, c.before(), s - 4)
                pe.wait_ge(dve_cm, (b + 1) * 4 * NU + RING)
                for k in range(KT):
                    mm = pe.matmul(PS[ROW_G1:ROW_G1 + HD, 0, :], WA[:, k, 3 * D:QW], xT[:, k, :], start=(k == 0),
                                   stop=(k == KT - 1), tile_position=(0, ROW_G1))
                mm.then_inc(pe_g1, 1)
                if m is not None:
                    chunk_run(m, C_BIAS[0], C_BIAS[0] + 1, 1)
                pe.wait_ge(act_g1, b + 1)
                for j in range(NT):
                    mm = pe.matmul(PS[:, 1 + j // 2, (j % 2) * D:(j % 2 + 1) * D], g1T[:, j * P:(j + 1) * P], WG2,
                                   start=True, stop=True, tile_position=(ROW_G1, 0))
                    if j % 2:
                        mm.then_inc(pe_g, 1)
                if m is not None:
                    chunk_run(m, C_BIAS[0] + 1, C_BIAS[1], 1)
                    for j in range(NT):
                        down(m, C_BIAS[1] - 1, j)
                settled_wait(pe, dve_bias, (b + 1) * NT)
                with pe.Fori(0, NG // 2) as i:
                    for u in range(2):
                        if u == 0:
                            pe.wait_ge(act_eg, (b + 1) * NT)
                        pe.wait_ge(act_eq2, b * NG + i * 2 + u + 1)
                        stack(EQ, 3 - 3 * u, i * 2 + u, pe_eq2)
                settled_wait(pe, act_eq2, (b + 1) * NG + 2)

                def units(i, first, last):
                    for u in range(first, last):
                        pe.wait_ge(act_p, b * 4 * NU + i * NU + u + 1)
                        score_unit(i, u, True)

                def outputs(i, u):
                    n = b * NG + i * 2 + u
                    pe.wait_ge(act_p, b * 4 * NU + i * NU + (u + 1) * NU // 2 + RING)
                    pe.wait_ge(pool_v, n + 1 + 1)
                    pe.wait_ge(dve_o, n + 1)
                    for t in range(NT):
                        for hh in range(HG):
                            o, w = POFF[t], S - P * t
                            mm = pe.matmul(PS[32 * hh:32 * hh + 32, BK_PV, t * P:S], vst[:, t, hh, :], PT[u][:, hh, o:o + w],
                                           start=(t == 0), stop=(t == NT - 1), tile_position=(0, 32 * hh))
                    mm.then_inc(pe_pv, 1)

                def to_tokens(i, u):
                    n = b * NG + i * 2 + u
                    pe.wait_ge(dve_o, n + 1 + 1)
                    pe.wait_ge(dve_otok, n + 1)
                    for j in range(NT):
                        mm = pe.transpose(PS[:, BK_OT, j * P:(j + 1) * P], osb[:, j * P:(j + 1) * P], ident)
                    mm.then_inc(pe_oT, 1)

                def prob_step(i, more):
                    units(i, RING, NU // 2 + RING)
                    outputs(i, 0)
                    units(i, NU // 2 + RING, NU)
                    to_tokens(i, 0)
                    if more:
                        units(i + 1, 0, RING)
                    outputs(i, 1)
                    to_tokens(i, 1)

                units(0, 0, RING)
                with pe.Fori(0, NG // 2 - 1) as i:
                    prob_step(i, True)
                prob_step(NG // 2 - 1, False)
                if m is not None:
                    pe.wait_ge(dve_otok, (b + 1) * NG + 1)
                    for c in range(*C_OUT):
                        for part in range(3):
                            up(m, c, part)
                        gate_of(m, c)
                        if c > C_OUT[0]:
                            for j in range(NT):
                                down(m, c - 1, j)
                    for j in range(NT):
                        down(m, NC - 1, j)
                pe.wait_ge(dve_on, b + 1)
                pe.wait_ge(act_p, (b + 1) * 4 * NU + RING)
                for k in range(KT):
                    for j in range(NT):
                        mm = pe.transpose(PS[:, k, j * P:(j + 1) * P], sq[:, j * H + 16 * k:j * H + 16 * k + 16, :].rearrange("p h d -> p (h d)"), ident)
                    mm.then_inc(pe_aT, 1)
                pe.wait_ge(act_aT, (b + 1) * KT)
                for j in range(NT):
                    for k in range(KT):
                        mm = pe.matmul(PS[:, 2 + j // 2, (j % 2) * D:(j % 2 + 1) * D], aT[:, k, j * P:(j + 1) * P],
                                       WO[:, k, :], start=(k == 0), stop=(k == KT - 1))
                    if j % 2:
                        mm.then_inc(pe_att, 1)

            class Routed:
                def __init__(self, value, static):
                    self.value, self.slot = value, static % 2

                def before(self):
                    r = Routed(self.value - 1, 0)
                    r.slot = 1 - self.slot
                    return r

            def up_r(m, c, part):
                up(m, c.value, part)

            def down_r(m, c, j):
                if j == 0:
                    pe.wait_ge(pool_hp, m * NC + c.value + 2)
                for a, e in ((0, 0), (0, 1), (1, 0)):
                    mm = pe.matmul(PS[:, BK_Y + j // 2, (j % 2) * D:(j % 2 + 1) * D], hp[:, c.slot, a, j * P:(j + 1) * P],
                                   W2[:, e, bass.ds(c.value, 1), :].rearrange("p o n -> p (o n)"), start=False, stop=False,
                                   skip_group_check=True)
                if j == NT - 1:
                    mm.then_inc(pe_y, 1)

            turn(0, None)
            with pe.Fori(1, B) as b:
                turn(b, b - 1)
            m = B - 1
            x1_transpose(m)
            router(m)
            for part in range(3):
                up(m, 0, part)
            gate_rows(m)
            open_outputs(m)
            chunk_run(m, 1, NC, 1)
            for j in range(NT):
                down(m, NC - 1, j)

        @block.scalar
        def _(act):
            for credit in (act_kz, act_eq, act_h):
                act.sem_inc(credit, 1)
            act.sem_inc(act_eq2, 2)
            act.wait_ge(s_const, 16 * (NCONST - 1))
            nc.scalar.activation(negm[:, 0:1], CF[:, 0:1], ACT.Exp).then_inc(act_p, RING)
            for n in range(2):
                act.wait_ge(s_w, 16 * (n + 1))
                nc.scalar.activation(W1[:, 0, n, :], (UK, UQ)[n][:, 0:FS + FR], ACT.Copy).then_inc(act_w, 1)
            for n, (c0, c1) in enumerate(((0, 13), (13, NC))):
                act.wait_ge(s_w, 16 * (n + 3))
                src = qf if n == 0 else kz[0][:, :, :].rearrange("p a s -> p (a s)").bitcast(F32)
                nc.scalar.activation(W2[:, 0, c0:c1, :].rearrange("p c n -> p (c n)"), src[:, 0:(c1 - c0) * D],
                                     ACT.Copy).then_inc(act_w, 1)
            nc.scalar.activation(CENT[:, 0], CENTF[:, :, :], ACT.Copy).then_inc(act_w, 1)

            def relu(m, c, slot):
                w = CHUNKS[c][1] if isinstance(c, int) else P
                act.wait_ge(pe_h, m * NC + c + 1)
                act.wait_ge(pool_hp, m * NC + c + 1)
                bias = b1[0:w, c:c + 1] if isinstance(c, int) else b1[:, bass.ds(c, 1)]
                nc.scalar.activation(hr[0:w, :], PS[0:w, BK_H, :], ACT.Relu, bias=bias).then_inc(act_h, 1)

            def high(m, c, slot):
                w = CHUNKS[c][1] if isinstance(c, int) else P
                if isinstance(c, int) and c < NSH:
                    act.wait_ge(act_h, m * NC + c + 2)
                else:
                    act.wait_ge(dve_h, m * (NC - NSH) + c - NSH + 2)
                act.wait_ge(pe_y, m * NC + c + 1)
                nc.scalar.activation(hp[0:w, slot, 0, :], hr[0:w, :], ACT.Copy).then_inc(act_hp, 1)

            def chunks(m, first, last):
                for c in range(first, last):
                    relu(m, c, c % 2)
                    high(m, c, c % 2)

            def x1T_parts(m):
                for k in range(KT):
                    act.wait_ge(pe_x1T, m * KT + k + 1)
                    if k == 0:
                        act.wait_ge(pe_y, m * NC + 2)
                    nc.scalar.activation(x1T[:, 0, k, :], PS[:, 4 + k, :], ACT.Copy).then_inc(act_x1T, 1)

            def route(m):
                act.wait_ge(pe_rt, m + 1)
                nc.scalar.activation(er[:, :, :].rearrange("p t e -> p (t e)"), PS[:, BK_Y, 0:NT * NE], ACT.Exp,
                                     scale=-1.0).then_inc(act_rt, 1)

            def gate_rows(m):
                act.wait_ge(pe_gT, m + 1)
                nc.scalar.activation(gTp, PSH[0:2 * NE, BK_Y + 1, 0:S], ACT.Copy).then_inc(act_gT, 1)
                nc.scalar.activation(gT, PS[ROW_GT:ROW_GT + NE + NS, BK_Y, :], ACT.Copy).then_inc(act_gT, 1)

            def turn(b, m):
                if m is not None:
                    x1T_parts(m)
                for j in range(NT):
                    act.wait_ge(pe_proj, b * NT + j + 1)
                    if j == 0:
                        act.wait_ge(pool_v, b * NG + 1)
                    nc.scalar.activation(v[:, j, :], PS[:, 2 + j % 2, 0:D], ACT.Copy).then_inc(act_v, 1)
                for j in range(NT):
                    act.wait_ge(dve_rope, b * NT + j + 1)
                    if j == 0:
                        act.wait_ge(pe_pv, b * NG + 2)
                    for E, c0, s0, step in ((EQ, 0, 0, 1), (EK, D, 0, 2)):
                        src = rot[:, j, c0:c0 + D].rearrange("p (h d) -> p h d", h=H).unsqueeze(2).to_broadcast([P, H, 2, HD])
                        dst = E[:, j, :, 0:CR].rearrange("p h (s d) -> p h s d", s=SLOTS)[:, :, s0:s0 + step + 1:step, :]
                        nc.scalar.activation(dst, src, ACT.Copy).then_inc(act_e, 1)
                if m is not None:
                    route(m)
                for k in range(KT):
                    act.wait_ge(pe_qT, b * KT + k + 1)
                    if k == 0:
                        act.wait_ge(dve_on, b)  if not isinstance(b, int) else None
                    nc.scalar.activation(qT[:, k, :], PS[:, k, :], ACT.Copy).then_inc(act_qT, 1)
                if m is not None:
                    chunks(m, 0, 1)
                    gate_rows(m)
                    chunks(m, 1, C_FIRST[1])
                    settled_wait(act, s_out, 16 * m + 16)
                with act.Fori(0, NG // 2) as i:
                    for u in range(2):
                        n = b * NG + i * 2 + u
                        if m is not None:
                            c = i * 2 + C_TOPK[0] + u
                            relu(m, c, (C_TOPK[0] + u) % 2)
                            high(m, c, (C_TOPK[0] + u) % 2)
                        act.wait_ge(pe_ek, n + 1)
                        for h in range(2):
                            nc.scalar.activation(kz[h][64 * h:64 * h + 64, bass.ds(i * 4 + u * 2, 2), :],
                                                 PSH[64 * h:64 * h + 64, 2, :].rearrange("p (a s) -> p a s", a=2),
                                                 ACT.Copy).then_inc(act_kz, 1)
                        act.wait_ge(pe_eq, n + 1)
                        nc.scalar.activation(qET[:, bass.ds(i * 4 + u * 2, 2), :],
                                             PSH[:, 3, :].rearrange("p (a s) -> p a s", a=2), ACT.Copy).then_inc(act_eq, 1)
                if m is not None:
                    with act.Fori(0, NG // 2) as i:
                        for u in range(2):
                            c = i * 2 + C_MAX[0] + u
                            relu(m, c, (C_MAX[0] + u) % 2)
                            high(m, c, (C_MAX[0] + u) % 2)
                act.wait_ge(pe_g1, b + 1)
                nc.scalar.activation(g1T, PS[ROW_G1:ROW_G1 + HD, 0, :], ACT.Copy).then_inc(act_g1, 1)
                if m is not None:
                    chunks(m, C_BIAS[0], C_BIAS[0] + 1)
                for j in range(NT):
                    act.wait_ge(pe_g, 2 * b + j // 2 + 1)
                    nc.scalar.activation(eg[:, j, :], PS[:, 1 + j // 2, (j % 2) * D:(j % 2 + 1) * D], ACT.Exp,
                                         scale=-1.0).then_inc(act_eg, 1)
                if m is not None:
                    chunks(m, C_BIAS[0] + 1, C_BIAS[1])
                act.wait_ge(pe_mx, (b + 1) * 4 * NU + 1)
                with act.Fori(0, NG // 2) as i:
                    for u in range(2):
                        act.wait_ge(pe_eq2, b * NG + i * 2 + u + 1 + 1)
                        nc.scalar.activation(qET[:, bass.ds(i * 4 + 2 * u, 2), :],
                                             PSH[:, 3 - 3 * u, :].rearrange("p (a s) -> p a s", a=2), ACT.Copy).then_inc(act_eq2, 1)
                with act.Fori(0, NG // 2) as i:
                    for u in range(NU):
                        half, s = divmod(u, NU // 2)
                        act.wait_ge(pe_sc, b * 4 * NU + i * NU + u + 1)
                        if s == 0:
                            act.wait_ge(pe_pv, b * NG + i * 2 + half + 1)
                        h0 = 2 * (s // 5)
                        if u % 5 == 2:
                            dst = PT[half][:, h0:h0 + 2, 1024:SW]
                            src = PS[:, u % RING, :].rearrange("p (a c) -> p a c", a=2)
                        else:
                            hh, o = h0 + (u % 5) // 3, 0 if u % 5 in (0, 3) else 512
                            dst, src = PT[half][:, hh, o:o + 512], PS[:, u % RING, :]
                        nc.scalar.activation(dst, src, ACT.Exp, scale=SCALE).then_inc(act_p, 1)
                if m is not None:
                    chunks(m, *C_OUT)
                for k in range(KT):
                    act.wait_ge(pe_aT, b * KT + k + 1)
                    nc.scalar.activation(aT[:, k, :], PS[:, k, :], ACT.Copy).then_inc(act_aT, 1)

            turn(0, None)
            with act.Fori(1, B) as b:
                turn(b, b - 1)
            m = B - 1
            x1T_parts(m)
            route(m)
            chunks(m, 0, 1)
            gate_rows(m)
            chunks(m, 1, NC)

        @block.gpsimd
        def _(pool):
            for credit in (pool_v, pool_e, pool_hp):
                pool.sem_inc(credit, 1)
            nc.gpsimd.memset(kz[1][:, :, :], 0.0).then_inc(s_one, 1)
            nc.gpsimd.memset(hp[:, :, :, :], 0.0)
            nc.gpsimd.memset(vst[:, :, :, :], 0.0)
            pool.drain()
            nc.gpsimd.memset(vst[:, :, :, HD:HD + 1], 1.0).then_inc(s_init, 1)
            pool.wait_ge(dve_w, 4)
            nc.gpsimd.memset(kz[0][:, :, :], 0.0).then_inc(s_init, 1)

            def low(m, c, slot):
                w = CHUNKS[c][1] if isinstance(c, int) else P
                pool.wait_ge(act_hp, m * NC + c + 1)
                nc.gpsimd.tensor_tensor(hp[0:w, slot, 1, :], hr[0:w, :], hp[0:w, slot, 0, :],
                                        ALU.subtract).then_inc(pool_hp, 1)

            def turn(b, m):
                settled_wait(pool, pe_pv, b * NG + 2)
                nc.gpsimd.memset(EQ[:, :, :, CR:HW], 0.0)
                nc.gpsimd.memset(EK[:, :, :, CR + NCH:HW], 0.0)
                for j in range(NT):
                    nc.gpsimd.tensor_scalar(EK[:, j, :, CR:CR + NCH], ind[:, j:j + 1, :].to_broadcast([P, H, NCH]),
                                            1.0, 0.0, ALU.mult, ALU.add)
                    for n, (E, c0, hi, lo, step) in enumerate(((EQ, 0, 0, 2, 1), (EK, D, 0, 1, 2))):
                        pool.wait_ge(act_e, (b * NT + j) * 2 + n + 1)
                        src = rot[:, j, c0:c0 + D].rearrange("p (h d) -> p h d", h=H).unsqueeze(2).to_broadcast([P, H, 2, HD])
                        e4 = E[:, j, :, 0:CR].rearrange("p h (s d) -> p h s d", s=SLOTS)
                        ins = nc.gpsimd.tensor_tensor(e4[:, :, lo:lo + step + 1:step, :], src,
                                                      e4[:, :, hi:hi + step + 1:step, :], ALU.subtract)
                    ins.then_inc(pool_e, 1)
                if m is not None:
                    for c in range(*C_FIRST):
                        low(m, c, c % 2)
                    for first, last in (C_TOPK, C_MAX):
                        pool.drain()
                        with pool.Fori(0, (last - first) // 2) as i:
                            for u in range(2):
                                low(m, i * 2 + first + u, (first + u) % 2)
                    for c in range(*C_BIAS):
                        low(m, c, c % 2)
                settled_wait(pool, act_v, (b + 1) * NT)
                with pool.Fori(0, NG) as g:
                    settled_wait(pool, pe_pv, b * NG + g + 2)
                    vg = v[:, :, bass.ds(g * HG * HD, HG * HD)].rearrange("p t (h d) -> p t h d", h=HG)
                    ones = vst[:, :, :, HD:HD + 1].to_broadcast([P, NT, HG, HD])
                    nc.gpsimd.tensor_tensor(vst[:, :, :, 0:HD], vg, ones, ALU.mult).then_inc(pool_v, 1)
                if m is not None:
                    for c in range(*C_OUT):
                        low(m, c, c % 2)

            turn(0, None)
            with pool.Fori(1, B) as b:
                turn(b, b - 1)
            for c in range(NC):
                low(B - 1, c, c % 2)

        @block.vector
        def _(dve):
            for credit in (dve_x1, dve_z, dve_o, dve_otok, dve_h):
                dve.sem_inc(credit, 1)
            dve.sem_inc(dve_cm, RING)
            dve.wait_ge(s_const, 16 * (NCONST - 1))
            nc.vector.memset(gmask[:, :, NCH:TOPW], PAD)
            nc.vector.memset(gext[:, :, NE:NE + NS], 1.0)
            nc.vector.memset(sc[:, :, NE:TOPW], PAD)
            nc.vector.tensor_tensor(rep[:, :, 0:NCH], gm_c[:, 0:1, :].to_broadcast([P, H, NCH]),
                                    sm_c[:, 0:1, :].to_broadcast([P, H, NCH]), ALU.max)
            dve.drain()
            nc.vector.tensor_scalar(cbias[:, 0], rep[:, :, 0:NCH], -OFF, None, ALU.max).then_inc(s_init, 1)
            for n in range(2):
                dve.wait_ge(act_w, n + 1)
                nc.vector.tensor_tensor(W1[:, 1, n, :], (UK, UQ)[n][:, 0:FS + FR], W1[:, 0, n, :], ALU.subtract).then_inc(dve_w, 1)
            for n, (c0, c1) in enumerate(((0, 13), (13, NC))):
                dve.wait_ge(act_w, n + 3)
                src = qf if n == 0 else kz[0][:, :, :].rearrange("p a s -> p (a s)").bitcast(F32)
                nc.vector.tensor_tensor(W2[:, 1, c0:c1, :].rearrange("p c n -> p (c n)"), src[:, 0:(c1 - c0) * D],
                                        W2[:, 0, c0:c1, :].rearrange("p c n -> p (c n)"), ALU.subtract).then_inc(dve_w, 1)
            dve.wait_ge(act_w, 5)
            nc.vector.tensor_tensor(CENT[:, 1], CENTF[:, :, :], CENT[:, 0], ALU.subtract).then_inc(dve_w, 1)
            nc.vector.tensor_scalar(WO[:, :, :], WO[:, :, :], onw, None, ALU.mult).then_inc(dve_w, 1)

            def link(ins):
                dve.drain()
                return ins

            def gated(m, c, slot):
                dve.wait_ge(pe_h, m * NC + c + 1)
                dve.wait_ge(act_h, m * NC + c + 2)
                nc.vector.tensor_tensor(hr[:, :], hr[:, :], PS[:, BK_G, :], ALU.mult).then_inc(dve_h, 1)

            def root(n):
                a, y, t = ms[:, 0:n], ry[:, 0:n], rt[:, 0:n]
                link(nc.vector.tensor_scalar(t.bitcast(I32), a.bitcast(I32), 1, None, ALU.logical_shift_right))
                link(nc.vector.tensor_scalar(y.bitcast(I32), t.bitcast(I32), -1.0, float(ROOT), ALU.mult, ALU.add))
                for _ in range(3):
                    link(nc.vector.tensor_tensor(t, y, y, ALU.mult))
                    link(nc.vector.scalar_tensor_tensor(out=t, in0=t, scalar=-0.5, in1=a, op0=ALU.mult, op1=ALU.mult))
                    link(nc.vector.scalar_tensor_tensor(out=y, in0=t, scalar=1.5, in1=y, op0=ALU.add, op1=ALU.mult))

            def layernorm(src, dst, done):
                for j in range(NT):
                    nc.vector.bn_stats(st6[:, j, :], src[:, j, :])
                dve.drain()
                for j in range(NT):
                    nc.vector.bn_aggr(mv[:, j, :], st6[:, j, :])
                dve.drain()
                link(nc.vector.tensor_scalar(ms[:, 0:NT], mv[:, :, 1], 1e-5, None, ALU.add))
                root(NT)
                for j in range(NT):
                    nc.vector.tensor_scalar(dst[:, j, :], src[:, j, :], mv[:, j, 0:1], ry[:, j:j + 1],
                                            ALU.subtract, ALU.mult).then_inc(done, 1)

            def x1T_parts(m):
                for k in range(KT):
                    dve.wait_ge(act_x1T, m * KT + k + 1)
                    nc.vector.tensor_tensor(x1T[:, 1, k, :], PS[:, 4 + k, :], x1T[:, 0, k, :], ALU.subtract).then_inc(dve_x1T, 1)

            def route(m):
                dve.wait_ge(act_rt, m + 1)
                link(nc.vector.tensor_scalar(er[:, :, :], er[:, :, :], 1.0, None, ALU.add))
                link(nc.vector.reciprocal(er[:, :, :], er[:, :, :]))
                link(nc.vector.tensor_tensor(sc[:, :, 0:NE], er[:, :, :], rbias.unsqueeze(1).to_broadcast([P, NT, NE]), ALU.add))
                for j in range(NT):
                    nc.vector.max(rtop[:, j, :], sc[:, j, 0:NE])
                dve.drain()
                link(nc.vector.memset(rtop[:, :, KR:8], PAD))
                for j in range(NT):
                    nc.vector.match_replace(rrep[:, j, :], rtop[:, j, :], sc[:, j, :], CHOSEN)
                dve.drain()
                link(nc.vector.scalar_tensor_tensor(out=gat[:, :, :], in0=rrep[:, :, 0:NE], scalar=BIG, in1=sc[:, :, 0:NE],
                                                    op0=ALU.is_gt, op1=ALU.mult))
                link(nc.vector.tensor_reduce(gsum[:, :], gat[:, :, :], AX.X, ALU.add))
                link(nc.vector.tensor_scalar(gsum[:, :], gsum[:, :], 1e-8, None, ALU.max))
                link(nc.vector.reciprocal(gsum[:, :], gsum[:, :]))
                gg = gext[:, :, 0:NE]
                link(nc.vector.tensor_tensor(gg, gat[:, :, :], gsum[:, :].unsqueeze(2).to_broadcast([P, NT, NE]), ALU.mult))
                link(nc.vector.tensor_copy(gsp[:, :, 0, :], gg))
                nc.vector.tensor_tensor(gsp[:, :, 1, :], gg, gsp[:, :, 0, :], ALU.subtract).then_inc(dve_g, 1)

            def finish(m):
                dve.wait_ge(pe_y, (m + 1) * NC + 2)
                for i in range(2):
                    xs = x1n[:, 2 * i:2 * i + 2, :].rearrange("p t d -> p (t d)")
                    nc.vector.scalar_tensor_tensor(out=xs, in0=xs, scalar=2.0, in1=PS[:, BK_Y + i, :],
                                                   op0=ALU.mult, op1=ALU.add).then_inc(dve_z, 1)
                dve.drain()
                settled_wait(dve, s_out, 16 * m + 16)
                layernorm(x1n, yout, dve_out)
                dve.drain()

            def turn(b, m):
                if m is not None:
                    x1T_parts(m)
                for j in range(NT):
                    dve.wait_ge(pe_proj, b * NT + j + 1)
                    if j == 0:
                        dve.wait_ge(pe_pv, b * NG + 2)
                        dve.wait_ge(pe_oT, b * NG + 1)
                    t = PS[:, j % 2, :].rearrange("p (h u f) -> p h u f", h=2 * H, u=2)
                    o = rot[:, j, :].rearrange("p (h u f) -> p h u f", h=2 * H, u=2)
                    w = ropeb[:, :].rearrange("p (h u f) -> p h u f", h=2 * H, u=2)
                    cj = cos[:, j:j + 1, :].to_broadcast([P, 2 * H, HD // 2])
                    sj = sin[:, j:j + 1, :].to_broadcast([P, 2 * H, HD // 2])
                    nc.vector.tensor_tensor(w[:, :, 0, :], t[:, :, 1, :], sj, ALU.mult)
                    nc.vector.tensor_tensor(w[:, :, 1, :], t[:, :, 0, :], sj, ALU.mult)
                    nc.vector.tensor_tensor(o[:, :, 0, :], t[:, :, 0, :], cj, ALU.mult)
                    link(nc.vector.tensor_tensor(o[:, :, 1, :], t[:, :, 1, :], cj, ALU.mult))
                    nc.vector.tensor_tensor(o[:, :, 0, :], o[:, :, 0, :], w[:, :, 0, :], ALU.subtract)
                    nc.vector.tensor_tensor(o[:, :, 1, :], o[:, :, 1, :], w[:, :, 1, :], ALU.add).then_inc(dve_rope, 1)
                    dve.drain()
                if m is not None:
                    route(m)
                dve.wait_ge(pe_km, b + 1 + 1)
                for k in range(KT):
                    nc.vector.tensor_tensor(
                        KB[:, k, :].rearrange("p (h n) -> p h n", n=NCH),
                        PS[:, 2, k * NCH:(k + 1) * NCH].unsqueeze(1).to_broadcast([P, 16, NCH]),
                        bmask.unsqueeze(2).to_broadcast([P, 16, NCH]), ALU.mult).then_inc(dve_kb, 1)
                c = C_TOPK[0]
                for j, bank in ((1, 3), (2, 0), (3, 1)):
                    dve.wait_ge(pe_gate, b * 3 + j + 1)
                    nc.vector.tensor_tensor(gmask[:, :, 0:NCH], PS[:, bank, :].rearrange("p (h n) -> p h n", n=NCH),
                                            gm_c[:, j:j + 1, :].to_broadcast([P, H, NCH]), ALU.add).then_inc(dve_gm, 1)
                    dve.drain()
                    for h in range(H):
                        nc.vector.max(top8[:, h, :], gmask[:, h, 0:NCH])
                    dve.drain()
                    link(nc.vector.memset(top8[:, :, TOPK - 1:8], PAD))
                    for q in range(4):
                        for h in range(8 * q, 8 * q + 8):
                            nc.vector.match_replace(rep[:, h, :], top8[:, h, :], gmask[:, h, :], CHOSEN)
                        if m is not None and c < C_TOPK[1] and q % 2:
                            gated(m, c, c % 2)
                            c += 1
                    dve.drain()
                    link(nc.vector.tensor_scalar(rep[:, :, 0:NCH], rep[:, :, 0:NCH], BIG, OFF, ALU.is_gt, ALU.mult))
                    link(nc.vector.tensor_tensor(rep[:, :, 0:NCH], rep[:, :, 0:NCH],
                                                 sm_c[:, j:j + 1, :].to_broadcast([P, H, NCH]), ALU.add))
                    link(nc.vector.tensor_scalar(cbias[:, j], rep[:, :, 0:NCH], -OFF, None, ALU.max))
                while m is not None and c < C_TOPK[1]:
                    gated(m, c, c % 2)
                    c += 1
                settled_wait(dve, pe_gate, (b + 1) * 3 + 1)
                with dve.Fori(0, NG // 2) as i:
                    for u in range(NU):
                        dve.wait_ge(pe_mx, b * 4 * NU + i * NU + u + 1 + 1)
                        h0 = i * 8 + 2 * (u // 5)
                        src = PS[:, u % RING, :].rearrange("p (c k) -> p c k", k=CHUNK)
                        if u % 5 == 2:
                            dst = CM[:, bass.ds(h0, 2), 32:40]
                            src = PS[:, u % RING, :].rearrange("p (a c k) -> p a c k", a=2, k=CHUNK)
                        else:
                            o = 0 if u % 5 in (0, 3) else 16
                            dst = CM[:, bass.ds(h0 + (u % 5) // 3, 1), o:o + 16].rearrange("p o c -> p (o c)")
                        nc.vector.tensor_reduce(dst, src, AX.X, ALU.max).then_inc(dve_cm, 1)
                        half, s = divmod(u, NU // 2)
                        if m is not None and s == 5:
                            gated(m, i * 2 + C_MAX[0] + half, (C_MAX[0] + half) % 2)
                dve.drain()
                for j in range(NT):
                    w = CPT * (j + 1)
                    link(nc.vector.scalar_tensor_tensor(out=rep[:, :, 0:w], in0=cbias[:, j, :, 0:w], scalar=UNIT,
                                                        in1=CM[:, :, MOFF[j] // CHUNK:MOFF[j] // CHUNK + w],
                                                        op0=ALU.mult, op1=ALU.add))
                    link(nc.vector.tensor_reduce(negm[:, :], rep[:, :, 0:w], AX.X, ALU.max, negate=True))
                    link(nc.vector.tensor_scalar(negm[:, :], negm[:, :], 1.0 / UNIT, None, ALU.mult))
                    if j == 0:
                        dve.wait_ge(pe_eq, (b + 1) * NG)
                    nc.vector.tensor_tensor(EQ[:, j, :, CR:CR + NCH], cbias[:, j],
                                            negm[:, :].unsqueeze(2).to_broadcast([P, H, NCH]), ALU.add).then_inc(dve_bias, 1)
                    dve.drain()
                    if m is not None and j < C_BIAS[1] - C_BIAS[0]:
                        gated(m, C_BIAS[0] + j, (C_BIAS[0] + j) % 2)
                with dve.Fori(0, NG) as g:
                    n = b * NG + g
                    dve.wait_ge(pe_pv, n + 1 + 2)
                    dve.wait_ge(pe_oT, n + 1)
                    nc.vector.tensor_copy(osb[:, :], PS[:, BK_PV, :]).then_inc(dve_o, 1)
                    dve.wait_ge(pe_oT, n + 1 + 1)
                    nc.vector.tensor_copy(
                        otok.rearrange("p (t h) d -> p t h d", t=NT)[:, :, bass.ds(g * HG, HG), :],
                        PS[:, BK_OT, :].rearrange("p (t h d) -> p t h d", t=NT, h=HG)[:, :, :, 0:HD + 1]).then_inc(dve_otok, 1)
                dve.drain()
                u8, s1 = otok[:, :, 0:HD], otok[:, :, HD]
                link(nc.vector.tensor_tensor(sq, u8, u8, ALU.mult))
                link(nc.vector.tensor_reduce(ms[:, :], sq, AX.X, ALU.add))
                link(nc.vector.tensor_tensor(rt[:, :], s1, s1, ALU.mult))
                link(nc.vector.scalar_tensor_tensor(out=ms[:, :], in0=rt[:, :], scalar=HD * 1e-6, in1=ms[:, :],
                                                    op0=ALU.mult, op1=ALU.add))
                link(nc.vector.tensor_scalar(ms[:, :], ms[:, :], 1.0 / HD, None, ALU.mult))
                root(NT * H)
                link(nc.vector.tensor_tensor(u8, u8, ry[:, :].unsqueeze(2).to_broadcast([P, NT * H, HD]), ALU.mult))
                dve.wait_ge(act_eg, (b + 1) * NT)
                e2 = eg.rearrange("p t d -> p (t d)")
                link(nc.vector.tensor_scalar(e2, e2, 1.0, None, ALU.add))
                if m is not None:
                    gated(m, C_OUT[0], C_OUT[0] % 2)
                link(nc.vector.reciprocal(e2, e2))
                if m is not None:
                    for c in range(C_OUT[0] + 1, C_OUT[1]):
                        gated(m, c, c % 2)
                nc.vector.tensor_tensor(sq, u8, e2.rearrange("p (h d) -> p h d", d=HD), ALU.mult).then_inc(dve_on, 1)
                if m is not None:
                    finish(m)
                dve.wait_ge(s_x, 16 * b + 16)
                for i in range(2):
                    dve.wait_ge(pe_att, 2 * b + i + 1)
                    nc.vector.tensor_tensor(x1n[:, 2 * i:2 * i + 2, :].rearrange("p t d -> p (t d)"), PS[:, 2 + i, :],
                                            x[:, 2 * i:2 * i + 2, :].rearrange("p t d -> p (t d)"), ALU.add).then_inc(dve_x1, 1)
                dve.drain()
                layernorm(x1n, x1n, dve_ln)

            turn(0, None)
            with dve.Fori(1, B) as b:
                turn(b, b - 1)
            m = B - 1
            x1T_parts(m)
            route(m)
            for c in range(NSH, NC):
                gated(m, c, c % 2)
            finish(m)


def kernel(**inputs):
    import numpy as np
    import ml_dtypes
    import concourse.bacc as bacc
    from concourse.bass_utils import run_bass_kernel_spmd as run

    a = {k[3:]: np.asarray(val) for k, val in inputs.items()}
    f32 = np.float32
    x = np.ascontiguousarray(a["attn_hidden_states"])
    cf = np.zeros((P, C_W), f32)
    p = np.arange(P)
    cf[:, C_ID:C_ID + P] = np.eye(P, dtype=f32)
    inv_freq = f32(1.0) / np.power(f32(10000.0), np.arange(0, HD, 2, dtype=f32) / f32(HD))
    freqs = np.arange(S, dtype=f32)[:, None] * inv_freq[None, :].astype(f32)
    tab = lambda t: t.astype(f32).reshape(NT, P, HD // 2).transpose(1, 0, 2).reshape(P, -1)
    cf[:, C_COS:C_COS + 16] = tab(np.cos(freqs))
    cf[:, C_SIN:C_SIN + 16] = tab(np.sin(freqs))
    cf[:, C_AVG:C_AVG + CPT] = (p[:, None] // CHUNK == np.arange(CPT)) / f32(CHUNK)
    cf[:, C_BM:C_BM + 16] = p[:, None] // HD == np.arange(16)
    own = (np.arange(NT)[None, :, None] * CPT + p[:, None, None] // CHUNK)
    n = np.arange(NCH)[None, None, :]
    cf[:, C_GM:C_GM + 64] = np.where(n < own, 0.0, -BIG).reshape(P, -1)
    cf[:, C_SM:C_SM + 64] = np.where(n == own, 0.0, -OFF).reshape(P, -1)
    ch = np.zeros((P, H_W), np.float16)
    ch[:, H_ID:H_ID + P] = np.eye(P)
    ch[:, H_IND:H_IND + 64] = np.where(n == own, UNIT, 0.0).reshape(P, -1)
    cg = np.zeros((P, G_W), f32)
    cg[:, G_ID:G_ID + P] = np.eye(P)
    cg[:, G_CQ:G_CQ + P] = np.where(p[None, :] > p[:, None], -BIG, 0.0)
    cg[:, G_CK:G_CK + P] = np.where(p[:, None] > p[None, :], -BIG, 0.0)
    one = np.tile((np.arange(FR) // DF)[None, :] == np.arange(NE)[:, None], (2, 1)).astype(np.float16)
    cf[:, C_ONW] = np.tile(a["attn_o_norm_weight"], P // HD)
    cf[:, C_RB:C_RB + NE] = a["ffn_bias"][None, :]
    b1 = np.concatenate([a["ffn_shared_b1"].reshape(-1), a["ffn_routed_b1"].reshape(-1)])
    w2f = np.concatenate([a["ffn_shared_w2"].reshape(-1, D), a["ffn_routed_w2"].reshape(-1, D)])
    w2 = np.zeros((NC * P, D), f32)
    for c, (f0, m) in enumerate(CHUNKS):
        cf[0:m, C_B1 + c] = b1[f0:f0 + m]
        w2[c * P:c * P + m] = w2f[f0:f0 + m]
    cols = lambda w: w.transpose(1, 0, 2).reshape(D, -1)
    arrays = {
        "in_xT": x.transpose(0, 2, 1),
        "in_x": x,
        "in_wa": np.concatenate([a["attn_Wq"].T, a["attn_Wk"].T, a["attn_Wv"].T, a["attn_Wg1"].T], axis=1),
        "in_wg2": a["attn_Wg2"].T,
        "in_wo": a["attn_Wo"].T,
        "in_w1": np.concatenate([cols(a["ffn_shared_w1"]), cols(a["ffn_routed_w1"])], axis=1),
        "in_w2": w2,
        "in_cent": a["ffn_centroids"].T,
        "in_b2": np.concatenate([a["ffn_routed_b2"], a["ffn_shared_b2"]]),
        "in_cf": cf,
        "in_ch": ch,
        "in_cg": cg.astype(ml_dtypes.bfloat16),
        "in_one": one,
    }
    arrays = {key: np.ascontiguousarray(val) for key, val in arrays.items()}
    nc = bacc.Bacc("TRN2", target_bir_lowering=False, num_devices=1)
    args = [nc.dram_tensor(key, val.shape, mybir.dt.from_np(val.dtype), kind="ExternalInput").ap()
            for key, val in arrays.items()]
    args.append(nc.dram_tensor("out", (B, S, D), F32, kind="ExternalOutput").ap())
    build(nc, *args)
    return run(nc, [arrays], core_ids=[0]).results[0]["out"]
```

```python
from contextlib import ExitStack

import concourse.bass as bass
from concourse import mybir
from concourse.alu_op_type import AluOpType as ALU

ACT = mybir.ActivationFunctionType
AX = mybir.AxisListType
F32 = mybir.dt.float32
F16 = mybir.dt.float16
BF16 = mybir.dt.bfloat16
I32 = mybir.dt.int32

P = 128
B, S, D = 8, 512, 256
H, HD = 32, 8
CHUNK, TOPK = 32, 4
NCH = S // CHUNK
NT = S // P
KT = D // P
CPT = P // CHUNK
HG = 4
NG = H // HG
SLOTS = 4
HW = 64
CR = SLOTS * HD
QW = D + D + D + HD
NE, NS, DF, KR = 16, 2, 176, 4
FS, FR = NS * DF, NE * DF
NSH = 3
CHUNKS = [(0, P), (P, P), (2 * P, FS - 2 * P)] + [(FS + P * i, P) for i in range(FR // P)]
NC = len(CHUNKS)
SCALE = HD ** -0.5
BIG = 1e30
PAD = -3e38
CHOSEN = 3e38
TOPW = NCH + 5
UNIT = 2.0 ** 15
OFF = 2.0 ** 15
ROOT = 0x5F3759DF
MOFF = {3: 0, 2: 512, 0: 896, 1: 1024}
POFF = {0: 0, 1: 512, 3: 896, 2: 1024}
SW = 1280
NU = 5
TU = NG * NU
RING = 2
C_FIRST, C_TOPK, C_MAX, C_BIAS = (0, 3), (3, 11), (11, 23), (23, 25)
MAX_STEPS = 2
MU = TU // MAX_STEPS
MC = (C_MAX[1] - C_MAX[0]) // MAX_STEPS
DEALT = [(c, part) for c in range(MC) for part in range(8)]


def dealt(u):
    return DEALT[u * len(DEALT) // MU:(u + 1) * len(DEALT) // MU]

C_ID, C_COS, C_SIN, C_AVG, C_BM, C_GM, C_SM, C_ONW, C_RB, C_B1 = 0, 128, 144, 160, 164, 180, 244, 308, 309, 325
C_W = C_B1 + NC
H_ID, H_IND, H_W = 0, 128, 192
G_ID, G_CQ, G_CK, G_W = 0, 128, 256, 384
ROW_G1, ROW_GT = 32, 64


def build(nc, xT_d, x_d, wa_d, wg2_d, wo_d, w1_d, w2_d, cent_d, b2_d, cf_d, ch_d, cg_d, one_d, out_d):
    with ExitStack() as ctx:
        def sb(name, shape, dt=F32):
            return ctx.enter_context(nc.sbuf_tensor(name, shape, dt))

        def sem(name):
            return ctx.enter_context(nc.semaphore(name))

        W1 = sb("W1", [P, 2, KT, FS + FR], F16)
        W2 = sb("W2", [P, 2, NC, D], F16)
        WA = sb("WA", [P, KT, QW])
        WO = sb("WO", [P, KT, D])
        CENT = sb("CENT", [P, 2, KT, NE], F16)
        ROWS = sb("ROWS", [P, FR], F16)
        B2 = ROWS[ROW_GT:ROW_GT + NE + NS, 0:2 * D].bitcast(F32)
        WG2 = ROWS[ROW_G1:ROW_G1 + HD, 0:2 * D].bitcast(F32)
        onehot = ROWS[0:2 * NE, :]
        CF = sb("CF", [P, C_W])
        CH = sb("CH", [P, H_W], F16)
        CG = sb("CG", [P, G_W], BF16)
        xT = sb("xT", [P, KT, S])
        UK = sb("UK", [P, 6144])
        UQ = sb("UQ", [P, HG * SW])
        EK = UK[:, 0:4096].bitcast(F16).rearrange("p (t h w) -> p t h w", t=NT, h=H)
        rot = UK[:, 4096:6144].rearrange("p (t c) -> p t c", t=NT)
        EQ = UQ[:, 0:4096].bitcast(F16).rearrange("p (t h w) -> p t h w", t=NT, h=H)
        PT = (UK[:, 0:HG * SW].rearrange("p (h w) -> p h w", h=HG),
              UQ[:, :].rearrange("p (h w) -> p h w", h=HG))
        ropeb = sb("ropeb", [P, 2 * D])
        KB = ropeb[:, :].rearrange("p (k d) -> p k d", k=KT)
        osb = ropeb
        v = sb("v", [P, NT, D])
        x = v
        qT = sb("qT", [P, KT, S])
        eg = qT[:, :, :].rearrange("p k s -> p (k s)").rearrange("p (t d) -> p t d", t=NT)
        gmask = sb("gmask", [P, H, TOPW])
        rep = sb("rep", [P, H, TOPW])
        cbias = sb("cbias", [P, NT, H, NCH], F16)
        qET = sb("qET", [P, H // 2, S], F16)
        qf = qET[:, :, :].rearrange("p a s -> p (a s)").bitcast(F32)
        aT = qf[:, 0:1024].rearrange("p (k s) -> p k s", k=KT)
        sq = qf[:, 2048:3072].rearrange("p (h d) -> p h d", d=HD)
        kz = (sb("kz0", [P, H // 2, S], F16),
              sb("kz1", [P, H // 2, S], F16))
        CM = sb("CM", [P, H, SW // CHUNK])
        cmf = CM[:, :, :].rearrange("p h c -> p (h c)")
        top8 = cmf[:, 0:H * 8].rearrange("p (h e) -> p h e", h=H)
        otok = cmf[:, 0:NT * H * (HD + 1)].rearrange("p (h d) -> p h d", d=HD + 1)
        vst = sb("vst", [P, NT, HG, 32])
        repf = rep[:, :, :].rearrange("p h w -> p (h w)")
        ms, ry, rt = (repf[:, n * NT * H:(n + 1) * NT * H] for n in range(3))
        st6 = repf[:, 3 * NT * H:3 * NT * H + NT * 6].rearrange("p (t s) -> p t s", t=NT)
        mv = repf[:, 3 * NT * H + NT * 6:3 * NT * H + NT * 8].rearrange("p (t s) -> p t s", t=NT)
        x1n = sb("x1n", [P, NT, D])
        x1T = sb("x1T", [P, 2, KT, S], F16)
        er = sb("er", [P, NT, NE])
        CENTF = er[:, 0:KT, :]
        sc = sb("sc", [P, NT, TOPW])
        rtop = sb("rtop", [P, NT, 8])
        rrep = sb("rrep", [P, NT, TOPW])
        gat = er
        negm = rtop[:, :, :].rearrange("p t e -> p (t e)")
        gsum = sb("gsum", [P, NT])
        gext = sb("gext", [P, NT, NE + NS])
        gsp = sb("gsp", [P, NT, 2, NE], F16)
        GR = sb("GR", [P, S])
        gT = GR[ROW_GT:ROW_GT + NE + NS, :]
        g1T = GR[ROW_G1:ROW_G1 + HD, :]
        gTp = GR[0:2 * NE, 0:S // 2].bitcast(F16)
        hr = sb("hr", [P, 2, S])
        hp = sb("hp", [P, 2, 2, S], F16)

        PS = ctx.enter_context(nc.psum_tensor("PS", [P, 8, 512], F32))
        PSH = PS[:, :, :].bitcast(F16)
        BK_H, BK_G, BK_Y = 4, 5, 6
        BK_PV, BK_OT = 4, 5

        ident = CF[:, C_ID:C_ID + P]
        cos = CF[:, C_COS:C_COS + 16].rearrange("p (t f) -> p t f", t=NT)
        sin = CF[:, C_SIN:C_SIN + 16].rearrange("p (t f) -> p t f", t=NT)
        avg = CF[:, C_AVG:C_AVG + CPT]
        bmask = CF[:, C_BM:C_BM + 16]
        gm_c = CF[:, C_GM:C_GM + 64].rearrange("p (t n) -> p t n", t=NT)
        sm_c = CF[:, C_SM:C_SM + 64].rearrange("p (t n) -> p t n", t=NT)
        onw = CF[:, C_ONW:C_ONW + 1]
        rbias = CF[:, C_RB:C_RB + NE]
        b1 = CF[:, C_B1:C_B1 + NC]
        identh = CH[:, H_ID:H_ID + P]
        ind = CH[:, H_IND:H_IND + 64].rearrange("p (t n) -> p t n", t=NT)
        identb = CG[:, G_ID:G_ID + P]
        causal_q = CG[:, G_CQ:G_CQ + P]
        causal_k = CG[:, G_CK:G_CK + P]

        s_const = sem("s_const")
        s_w = [sem(f"s_w{n}") for n in range(4)]
        s_init = sem("s_init")
        s_one = sem("s_one")
        act_w = sem("act_w")
        dve_w = sem("dve_w")
        s_xT = sem("s_xT")
        s_x = sem("s_x")
        s_out = sem("s_out")
        pe_proj = sem("pe_proj")
        dve_rope = sem("dve_rope")
        act_v = sem("act_v")
        act_e = sem("act_e")
        pool_e = sem("pool_e")
        pe_qT = sem("pe_qT")
        act_qT = sem("act_qT")
        pe_km = sem("pe_km")
        dve_kb = sem("dve_kb")
        pe_gate = sem("pe_gate")
        dve_gm = sem("dve_gm")
        pe_ek = sem("pe_ek")
        act_kz = sem("act_kz")
        pe_eq = sem("pe_eq")
        act_eq = sem("act_eq")
        pe_mx = sem("pe_mx")
        dve_cm = sem("dve_cm")
        dve_bias = sem("dve_bias")
        pe_eq2 = sem("pe_eq2")
        act_eq2 = sem("act_eq2")
        dve_eq2 = sem("dve_eq2")
        pe_g1 = sem("pe_g1")
        act_g1 = sem("act_g1")
        pe_g = sem("pe_g")
        act_eg = sem("act_eg")
        pe_sc = sem("pe_sc")
        act_p = sem("act_p")
        pool_v = sem("pool_v")
        pe_pv = sem("pe_pv")
        dve_o = sem("dve_o")
        pe_oT = sem("pe_oT")
        dve_otok = sem("dve_otok")
        dve_on = sem("dve_on")
        pe_aT = sem("pe_aT")
        act_aT = sem("act_aT")
        pe_att = sem("pe_att")
        dve_x1 = sem("dve_x1")
        dve_ln = sem("dve_ln")
        pe_x1T = sem("pe_x1T")
        act_x1T = sem("act_x1T")
        dve_x1T = sem("dve_x1T")
        pe_rt = sem("pe_rt")
        act_rt = sem("act_rt")
        dve_g = sem("dve_g")
        pe_gT = sem("pe_gT")
        act_gT = sem("act_gT")
        pe_h = sem("pe_h")
        act_h = sem("act_h")
        dve_h = sem("dve_h")
        act_hp = sem("act_hp")
        pool_hp = sem("pool_hp")
        pe_y = sem("pe_y")
        dve_z = sem("dve_z")
        dve_out = sem("dve_out")

        def settled_wait(eng, which, count):
            if not isinstance(count, int):
                count = eng.to_reg(count)
                eng.wait_ge(s_one, 1)
            eng.wait_ge(which, count)

        block = ctx.enter_context(nc.Block())
        NCONST = 10

        @block.sync
        def _(sp):
            sp.sem_inc(s_out, 16)
            sp.dma_start(xT[:, :, :], xT_d[0:1].rearrange("o (k p) s -> p (o k) s", p=P)).then_inc(s_xT, 16)
            for dst, src in ((CF[:, :], cf_d), (CH[:, :], ch_d), (CG[:, :], cg_d),
                             (WA[:, :, :], wa_d.rearrange("(k p) n -> p k n", p=P)),
                             (WG2, wg2_d), (B2, b2_d), (onehot, one_d),
                             (WO[:, :, :], wo_d.rearrange("(k p) n -> p k n", p=P)),
                             (CENTF[:, :, :], cent_d.rearrange("(k p) n -> p k n", p=P))):
                sp.dma_start(dst, src).then_inc(s_const, 16)
            w1_v = w1_d.rearrange("(k p) n -> k p n", p=P)
            w2_v = w2_d.rearrange("(c p) n -> p c n", p=P)
            k0f = kz[0][:, :, :].rearrange("p a s -> p (a s)").bitcast(F32)
            sp.dma_start(UK[:, 0:FS + FR], w1_v[0]).then_inc(s_w[0], 16)
            sp.dma_start(UQ[:, 0:FS + FR], w1_v[1]).then_inc(s_w[1], 16)
            sp.dma_start(qf[:, 0:13 * D].rearrange("p (c n) -> p c n", n=D), w2_v[:, 0:13]).then_inc(s_w[2], 16)
            sp.dma_start(k0f[:, 0:12 * D].rearrange("p (c n) -> p c n", n=D), w2_v[:, 13:NC]).then_inc(s_w[3], 16)

            def load_xT(b):
                sp.dma_start(xT[:, :, :], xT_d[bass.ds(b, 1)].rearrange("o (k p) s -> p (o k) s", p=P)).then_inc(s_xT, 16)

            def load_x(b):
                settled_wait(sp, pool_v, (b + 1) * NG + 1)
                sp.dma_start(x[:, :, :], x_d[bass.ds(b, 1)].rearrange("o (t p) d -> p (o t) d", p=P)).then_inc(s_x, 16)

            def store(b):
                settled_wait(sp, dve_out, (b + 1) * NT)
                sp.dma_start(out_d[bass.ds(b, 1)].rearrange("o (t p) d -> p (o t) d", p=P), x1n[:, :, :]).then_inc(s_out, 16)

            sp.wait_ge(pe_g1, 1)
            load_xT(1)
            load_x(0)
            with sp.Fori(1, B - 1) as b:
                settled_wait(sp, pe_g1, b + 1)
                load_xT(b + 1)
                store(b - 1)
                load_x(b)
            store(B - 2)
            load_x(B - 1)
            store(B - 1)
            sp.wait_ge(s_out, 16 * B + 16)

        @block.tensor
        def _(pe):
            for credit in (pe_eq2, pe_km, pe_gate, pe_mx, pe_oT):
                pe.sem_inc(credit, 1)
            pe.sem_inc(pe_y, 2)
            pe.sem_inc(pe_pv, 2)
            pe.wait_ge(s_const, 16 * (NCONST - 1))

            def project(b):
                pe.wait_ge(s_xT, 16 * b + 16)
                for j in range(NT):
                    for k in range(KT):
                        pe.matmul(PS[:, j, :], xT[:, k, j * P:(j + 1) * P], WA[:, k, 0:2 * D],
                                  start=(k == 0), stop=(k == KT - 1))
                    for k in range(KT):
                        mm = pe.matmul(PS[:, BK_Y + j // 2, (j % 2) * D:(j % 2 + 1) * D], xT[:, k, j * P:(j + 1) * P],
                                       WA[:, k, 2 * D:3 * D], start=(k == 0), stop=(k == KT - 1))
                    mm.then_inc(pe_proj, 1)

            def chunk_means(b):
                pe.wait_ge(dve_rope, (b + 1) * NT)
                for m in range(KT):
                    for j in range(NT):
                        mm = pe.transpose(PS[:, m, j * P:(j + 1) * P], rot[:, j, m * P:(m + 1) * P], ident)
                    mm.then_inc(pe_qT, 1)
                for m in range(KT):
                    for j in range(NT):
                        mm = pe.matmul(PS[:, 2, m * NCH + j * CPT:m * NCH + (j + 1) * CPT],
                                       rot[:, j, D + m * P:D + (m + 1) * P], avg, start=True, stop=True)
                mm.then_inc(pe_km, 1)

            def chunk_gates(b):
                pe.wait_ge(act_qT, (b + 1) * KT)
                pe.wait_ge(dve_kb, (b + 1) * KT)
                for j, bank in ((1, 3), (2, 0), (3, 1)):
                    for m in range(KT):
                        mm = pe.matmul(PS[:, bank, m * D:(m + 1) * D], qT[:, m, j * P:(j + 1) * P], KB[:, m, :],
                                       start=True, stop=True)
                    mm.then_inc(pe_gate, 1)

            def stack(E, bank, g, done):
                for j in range(NT):
                    for pr in range(2):
                        mm = pe.transpose(PSH[:, bank, pr * S + j * P:pr * S + (j + 1) * P],
                                          E[:, j, bass.ds(g * HG + 2 * pr, 2), :].rearrange("p h w -> p (h w)"), identh)
                mm.then_inc(done, 1)

            def score_unit(g, r, d, by_key):
                flat = PS[:, 2 * r:2 * r + 2, :].rearrange("p a c -> p (a c)")
                off, wide = (POFF, (0, 1, 3)) if by_key else (MOFF, (3, 2, 0))
                narrow = 2 if by_key else 1
                blocks = [(d, t, off[t]) for t in wide] if d < HG else [(h, narrow, h * 256) for h in range(HG)]
                for h, t, o in blocks:
                    pair = bass.ds(g * 2 + h // 2, 1)
                    if by_key:
                        w, diag = S - P * t, o
                        lhsT, rhs = kz[h % 2][:, pair, t * P:(t + 1) * P], qET[:, pair, t * P:S]
                    else:
                        w, diag = P * (t + 1), o + P * t
                        lhsT, rhs = qET[:, pair, t * P:(t + 1) * P], kz[h % 2][:, pair, 0:w]
                    pe.matmul(flat[:, o:o + w], lhsT.rearrange("p o s -> p (o s)"), rhs.rearrange("p o s -> p (o s)"),
                              start=True, stop=False)
                    mm = pe.matmul(flat[:, diag:diag + P], identb, causal_k if by_key else causal_q, start=False, stop=True)
                mm.then_inc(pe_sc if by_key else pe_mx, 1)

            def x1_transpose(m):
                pe.wait_ge(dve_ln, (m + 1) * NT)
                for k in range(KT):
                    for j in range(NT):
                        mm = pe.transpose(PS[:, 4 + k, j * P:(j + 1) * P], x1n[:, j, k * P:(k + 1) * P], ident)
                    mm.then_inc(pe_x1T, 1)

            def router(m):
                pe.wait_ge(dve_z, 2 * m + 1)
                pe.wait_ge(act_x1T, (m + 1) * KT)
                pe.wait_ge(dve_x1T, (m + 1) * KT)
                pe.wait_ge(act_v, 2 * min(m + 2, B) if isinstance(m, int) else 2 * m + 4)
                for j in range(NT):
                    for n, (k, a, c) in enumerate((k, a, c) for k in range(KT) for a, c in ((0, 0), (0, 1), (1, 0))):
                        mm = pe.matmul(PS[:, BK_Y, j * NE:(j + 1) * NE], x1T[:, a, k, j * P:(j + 1) * P], CENT[:, c, k, :],
                                       start=(n == 0), stop=(n == 3 * KT - 1))
                mm.then_inc(pe_rt, 1)

            def gate_rows(m):
                settled_wait(pe, dve_g, m + 1)
                for j in range(NT):
                    pe.transpose(PSH[0:2 * NE, BK_Y + 1, j * P:(j + 1) * P], gsp[:, j].rearrange("p a e -> p (a e)"), identh)
                for j in range(NT):
                    mm = pe.matmul(PS[ROW_GT:ROW_GT + NE + NS, BK_Y, j * P:(j + 1) * P], gext[:, j, :], ident, start=True, stop=True,
                                   tile_position=(0, ROW_GT))
                mm.then_inc(pe_gT, 1)

            def open_outputs(m):
                pe.wait_ge(act_gT, 2 * m + 2)
                for j in range(NT):
                    pe.matmul(PS[:, BK_Y + j // 2, (j % 2) * D:(j % 2 + 1) * D], gT[:, j * P:(j + 1) * P], B2,
                              start=(j % 2 == 0), stop=False, skip_group_check=True, tile_position=(ROW_GT, 0))

            def hidden_cols(c):
                return CHUNKS[c] if isinstance(c, int) else (FS + (c - NSH) * P, P)

            def up(m, c, part):
                f0, w = hidden_cols(c)
                if part == 0:
                    pe.wait_ge(act_h, m * NC + c + 1)
                for n in (2 * part, 2 * part + 1):
                    k, (a, e) = n // 3, ((0, 0), (0, 1), (1, 0))[n % 3]
                    mm = pe.matmul(PS[0:w, BK_H, :], W1[:, a, k, bass.ds(f0, w)], x1T[:, e, k, :],
                                   start=(n == 0), stop=(n == 5))
                if part == 2 and isinstance(c, int) and c < NSH:
                    mm.then_inc(pe_h, 1)

            def gate_of(m, c):
                pe.wait_ge(dve_h, m * (NC - NSH) + c - NSH + 1)
                pe.matmul(PS[:, BK_G, :], onehot[:, bass.ds((c - NSH) * P, P)], gTp, start=True, stop=True).then_inc(pe_h, 1)

            def down(m, c, j):
                w = CHUNKS[c][1] if isinstance(c, int) else P
                if j == 0:
                    pe.wait_ge(pool_hp, m * NC + c + 3)
                cc = c if isinstance(c, int) else c
                for a, e in ((0, 0), (0, 1), (1, 0)):
                    last = isinstance(c, int) and c == NC - 1 and (a, e) == (1, 0)
                    slot = c % 2 if isinstance(c, int) else None
                    mm = pe.matmul(PS[:, BK_Y + j // 2, (j % 2) * D:(j % 2 + 1) * D],
                                   hp[0:w, slot, a, j * P:(j + 1) * P],
                                   W2[0:w, e, cc, :], start=False, stop=last, skip_group_check=True)
                if j == NT - 1:
                    mm.then_inc(pe_y, 1)

            def chunk_run(m, first, last, lag):
                for c in range(first, last):
                    for part in range(3):
                        up(m, c, part)
                    if c >= NSH:
                        gate_of(m, c)
                    if c > 0:
                        for j in range(NT):
                            down(m, c - 1, j)

            def turn(b, m, more):
                if m is not None:
                    x1_transpose(m)
                    router(m)
                for k in range(KT):
                    mm = pe.matmul(PS[ROW_G1:ROW_G1 + HD, BK_G, :], WA[:, k, 3 * D:QW], xT[:, k, :], start=(k == 0),
                                   stop=(k == KT - 1), tile_position=(0, ROW_G1))
                mm.then_inc(pe_g1, 1)
                chunk_means(b)
                if m is not None:
                    for part in range(3):
                        up(m, 0, part)
                chunk_gates(b)
                if m is not None:
                    for part in range(3):
                        up(m, 1, part)
                    gate_rows(m)
                    open_outputs(m)
                    for part in range(3):
                        up(m, 2, part)
                    for c in (0, 1):
                        for j in range(NT):
                            down(m, c, j)
                if m is None:
                    pe.wait_ge(s_init, 3)
                    pe.wait_ge(act_w, 5)
                    pe.wait_ge(dve_w, 6)
                pe.wait_ge(act_g1, b + 1)
                settled_wait(pe, dve_gm, b * 3 + 1)
                with pe.Fori(0, NG // 2) as i:
                    for u in range(2):
                        n = b * NG + i * 2 + u
                        if m is not None:
                            c = Routed(i * 2 + C_TOPK[0] + u, u + C_TOPK[0])
                            for part in range(3):
                                up_r(m, c, part)
                            gate_of(m, c.value)
                        if u == 0:
                            pe.wait_ge(pool_e, (b + 1) * NT + 1)
                        pe.wait_ge(act_kz, 2 * n + 1)
                        stack(EK, 2, i * 2 + u, pe_ek)
                        pe.wait_ge(act_eq, n + 1)
                        stack(EQ, 3, i * 2 + u, pe_eq)
                        if m is not None:
                            for j in range(NT):
                                down_r(m, c.before(), j)
                pe.wait_ge(act_kz, (b + 1) * 2 * NG + 1)
                pe.wait_ge(act_eq, (b + 1) * NG + 1)
                settled_wait(pe, dve_gm, (b + 1) * 3)
                with pe.Fori(0, MAX_STEPS) as i:
                    for u in range(MU):
                        pe.wait_ge(dve_cm, b * TU + i * MU + u + 1)
                        score_unit(i * (NG // MAX_STEPS) + u // NU, u % RING, u % NU, False)
                        for cc, part in dealt(u) if m is not None else ():
                            c = Routed(i * MC + C_MAX[0] + cc, cc + C_MAX[0])
                            if part < 3:
                                up_r(m, c, part)
                            elif part == 3:
                                gate_of(m, c.value)
                            else:
                                down_r(m, c.before(), part - 4)
                pe.wait_ge(dve_cm, (b + 1) * TU + RING)
                for j in range(NT):
                    mm = pe.matmul(PS[:, j // 2, (j % 2) * D:(j % 2 + 1) * D], g1T[:, j * P:(j + 1) * P], WG2,
                                   start=True, stop=True, tile_position=(ROW_G1, 0))
                    if j % 2:
                        mm.then_inc(pe_g, 1)
                if m is not None:
                    chunk_run(m, *C_BIAS, 1)
                settled_wait(pe, dve_bias, (b + 1) * NT)
                with pe.Fori(0, NG // 4) as i:
                    for u in range(4):
                        if u == 2:
                            pe.wait_ge(act_eg, 2 * b + 2)
                        pe.wait_ge(dve_eq2 if u % 2 else act_eq2, b * (NG // 2) + i * 2 + u // 2 + 1)
                        stack(EQ, (2, 3, 0, 1)[u], i * 4 + u, pe_eq2)
                if m is not None:
                    for j in range(NT):
                        down(m, NC - 1, j)
                pe.wait_ge(act_eq2, (b + 1) * (NG // 2) + 2)
                settled_wait(pe, dve_eq2, (b + 1) * (NG // 2) + 2)

                def unit(g, gs, d):
                    pe.wait_ge(act_p, b * TU + g * NU + d + 1)
                    score_unit(g, (gs * NU + d) % RING, d, True)

                def outputs(g, gs, t):
                    if t == 0:
                        pe.wait_ge(act_p, b * TU + (g + 1) * NU + RING)
                        pe.wait_ge(pool_v, b * NG + g + 1 + 1)
                        pe.wait_ge(dve_o, b * NG + g + 1)
                    o, w = POFF[t], S - P * t
                    for hh in range(HG):
                        mm = pe.matmul(PS[32 * hh:32 * hh + 32, BK_PV, t * P:S], vst[:, t, hh, :], PT[gs % 2][:, hh, o:o + w],
                                       start=(t == 0), stop=(t == NT - 1), tile_position=(0, 32 * hh))
                    if t == NT - 1:
                        mm.then_inc(pe_pv, 1)

                def to_tokens(g):
                    n = b * NG + g
                    pe.wait_ge(dve_o, n + 1 + 1)
                    pe.wait_ge(dve_otok, n + 1)
                    for j in range(NT):
                        mm = pe.transpose(PS[:, BK_OT, j * P:(j + 1) * P], osb[:, j * P:(j + 1) * P], ident)
                    mm.then_inc(pe_oT, 1)

                def group(g, gs):
                    unit(g, gs, 0)
                    unit(g, gs, 1)
                    if gs > 1:
                        to_tokens(g - 2)
                    for t in range(NT):
                        outputs(g - 1, gs - 1, t)
                        if t + 2 < NU:
                            unit(g, gs, t + 2)

                for d in range(NU):
                    unit(0, 0, d)
                group(1, 1)
                with pe.Fori(0, NG // 2 - 1) as i:
                    for u in range(2):
                        group(i * 2 + 2 + u, 2 + u)
                if more:
                    pe.wait_ge(act_p, (b + 1) * TU + RING)
                to_tokens(NG - 2)
                for t in range(NT):
                    outputs(NG - 1, NG - 1, t)
                if more:
                    if m is not None:
                        pe.wait_ge(dve_z, 2 * m + 3)
                    project(b + 1)
                to_tokens(NG - 1)
                pe.wait_ge(dve_on, b + 1)
                for k in range(KT):
                    for j in range(NT):
                        mm = pe.transpose(PS[:, 4 + k, j * P:(j + 1) * P], sq[:, j * H + 16 * k:j * H + 16 * k + 16, :].rearrange("p h d -> p (h d)"), ident)
                    mm.then_inc(pe_aT, 1)
                pe.wait_ge(act_aT, (b + 1) * KT)
                for j in range(NT):
                    for k in range(KT):
                        mm = pe.matmul(PS[:, 4 + j // 2, (j % 2) * D:(j % 2 + 1) * D], aT[:, k, j * P:(j + 1) * P],
                                       WO[:, k, :], start=(k == 0), stop=(k == KT - 1))
                    if j % 2:
                        mm.then_inc(pe_att, 1)

            class Routed:
                def __init__(self, value, static):
                    self.value, self.slot = value, static % 2

                def before(self):
                    r = Routed(self.value - 1, 0)
                    r.slot = 1 - self.slot
                    return r

            def up_r(m, c, part):
                up(m, c.value, part)

            def down_r(m, c, j):
                if j == 0:
                    pe.wait_ge(pool_hp, m * NC + c.value + 3)
                for a, e in ((0, 0), (0, 1), (1, 0)):
                    mm = pe.matmul(PS[:, BK_Y + j // 2, (j % 2) * D:(j % 2 + 1) * D], hp[:, c.slot, a, j * P:(j + 1) * P],
                                   W2[:, e, bass.ds(c.value, 1), :].rearrange("p o n -> p (o n)"), start=False, stop=False,
                                   skip_group_check=True)
                if j == NT - 1:
                    mm.then_inc(pe_y, 1)

            project(0)
            turn(0, None, True)
            with pe.Fori(1, B - 1) as b:
                turn(b, b - 1, True)
            turn(B - 1, B - 2, False)
            m = B - 1
            x1_transpose(m)
            router(m)
            for c in (0, 1):
                for part in range(3):
                    up(m, c, part)
            gate_rows(m)
            open_outputs(m)
            for j in range(NT):
                down(m, 0, j)
            chunk_run(m, 2, NC, 1)
            for j in range(NT):
                down(m, NC - 1, j)

        @block.scalar
        def _(act):
            for credit in (act_kz, act_eq, act_h):
                act.sem_inc(credit, 1)
            act.sem_inc(act_eq2, 2)
            act.wait_ge(s_const, 16 * (NCONST - 1))
            nc.scalar.activation(hr[:, 0, 0:1], CF[:, 0:1], ACT.Exp).then_inc(act_p, RING)
            for n in range(2):
                act.wait_ge(s_w[n], 16)
                nc.scalar.activation(W1[:, 0, n, :], (UK, UQ)[n][:, 0:FS + FR], ACT.Copy).then_inc(act_w, 1)
            for n, (c0, c1) in enumerate(((0, 13), (13, NC))):
                act.wait_ge(s_w[n + 2], 16)
                src = qf if n == 0 else kz[0][:, :, :].rearrange("p a s -> p (a s)").bitcast(F32)
                nc.scalar.activation(W2[:, 0, c0:c1, :].rearrange("p c n -> p (c n)"), src[:, 0:(c1 - c0) * D],
                                     ACT.Copy).then_inc(act_w, 1)
            nc.scalar.activation(CENT[:, 0], CENTF[:, :, :], ACT.Copy).then_inc(act_w, 1)

            def relu(m, c, slot):
                w = CHUNKS[c][1] if isinstance(c, int) else P
                act.wait_ge(pe_h, m * NC + c + 1)
                act.wait_ge(pool_hp, m * NC + c + 1)
                bias = b1[0:w, c:c + 1] if isinstance(c, int) else b1[:, bass.ds(c, 1)]
                nc.scalar.activation(hr[0:w, slot, :], PS[0:w, BK_H, :], ACT.Relu, bias=bias).then_inc(act_h, 1)

            def high(m, c, slot):
                w = CHUNKS[c][1] if isinstance(c, int) else P
                if isinstance(c, int) and c < NSH:
                    act.wait_ge(act_h, m * NC + c + 2)
                else:
                    act.wait_ge(dve_h, m * (NC - NSH) + c - NSH + 2)
                act.wait_ge(pe_y, m * NC + c + 1)
                nc.scalar.activation(hp[0:w, slot, 0, :], hr[0:w, slot, :], ACT.Copy).then_inc(act_hp, 1)

            def chunks(m, first, last):
                for c in range(first, last):
                    relu(m, c, c % 2)
                    high(m, c, c % 2)

            def x1T_parts(m):
                for k in range(KT):
                    act.wait_ge(pe_x1T, m * KT + k + 1)
                    if k == 0:
                        act.wait_ge(pe_y, m * NC + 2)
                    nc.scalar.activation(x1T[:, 0, k, :], PS[:, 4 + k, :], ACT.Copy).then_inc(act_x1T, 1)

            def route(m):
                act.wait_ge(pe_rt, m + 1)
                nc.scalar.activation(er[:, :, :].rearrange("p t e -> p (t e)"), PS[:, BK_Y, 0:NT * NE], ACT.Exp,
                                     scale=-1.0).then_inc(act_rt, 1)

            def gate_rows(m):
                act.wait_ge(pe_gT, m + 1)
                nc.scalar.activation(gTp, PSH[0:2 * NE, BK_Y + 1, 0:S], ACT.Copy).then_inc(act_gT, 1)
                nc.scalar.activation(gT, PS[ROW_GT:ROW_GT + NE + NS, BK_Y, :], ACT.Copy).then_inc(act_gT, 1)

            def turn(b, m):
                for i in range(2):
                    act.wait_ge(pe_proj, b * NT + 2 * i + 2)
                    if i == 0:
                        act.wait_ge(dve_x1, 2 * b + 1)
                    nc.scalar.activation(v[:, 2 * i:2 * i + 2, :].rearrange("p t d -> p (t d)"), PS[:, BK_Y + i, :],
                                         ACT.Copy).then_inc(act_v, 1)
                if m is not None:
                    x1T_parts(m)
                for j in range(NT):
                    act.wait_ge(dve_rope, b * NT + j + 1)
                    if j == 0:
                        act.wait_ge(pe_pv, b * NG + 2)
                    for E, c0, s0, step in ((EQ, 0, 0, 1), (EK, D, 0, 2)):
                        src = rot[:, j, c0:c0 + D].rearrange("p (h d) -> p h d", h=H).unsqueeze(2).to_broadcast([P, H, 2, HD])
                        dst = E[:, j, :, 0:CR].rearrange("p h (s d) -> p h s d", s=SLOTS)[:, :, s0:s0 + step + 1:step, :]
                        nc.scalar.activation(dst, src, ACT.Copy).then_inc(act_e, 1)
                if m is not None:
                    route(m)
                act.wait_ge(pe_g1, b + 1)
                nc.scalar.activation(g1T, PS[ROW_G1:ROW_G1 + HD, BK_G, :], ACT.Copy).then_inc(act_g1, 1)
                for k in range(KT):
                    act.wait_ge(pe_qT, b * KT + k + 1)
                    if k == 0:
                        act.wait_ge(dve_on, b)  if not isinstance(b, int) else None
                    nc.scalar.activation(qT[:, k, :], PS[:, k, :], ACT.Copy).then_inc(act_qT, 1)
                if m is not None:
                    chunks(m, 0, 2)
                    gate_rows(m)
                    chunks(m, 2, C_FIRST[1])
                with act.Fori(0, NG // 2) as i:
                    for u in range(2):
                        n = b * NG + i * 2 + u
                        if m is not None:
                            c = i * 2 + C_TOPK[0] + u
                            relu(m, c, (C_TOPK[0] + u) % 2)
                        act.wait_ge(pe_ek, n + 1)
                        for h in range(2):
                            nc.scalar.activation(kz[h][64 * h:64 * h + 64, bass.ds(i * 4 + u * 2, 2), :],
                                                 PSH[64 * h:64 * h + 64, 2, :].rearrange("p (a s) -> p a s", a=2),
                                                 ACT.Copy).then_inc(act_kz, 1)
                        act.wait_ge(pe_eq, n + 1)
                        nc.scalar.activation(qET[:, bass.ds(i * 4 + u * 2, 2), :],
                                             PSH[:, 3, :].rearrange("p (a s) -> p a s", a=2), ACT.Copy).then_inc(act_eq, 1)
                        if m is not None:
                            high(m, c, (C_TOPK[0] + u) % 2)
                if m is not None:
                    with act.Fori(0, MAX_STEPS) as i:
                        for u in range(MC):
                            c = i * MC + C_MAX[0] + u
                            relu(m, c, (C_MAX[0] + u) % 2)
                            high(m, c, (C_MAX[0] + u) % 2)
                for i in range(2):
                    act.wait_ge(pe_g, 2 * b + i + 1)
                    nc.scalar.activation(eg[:, 2 * i:2 * i + 2, :].rearrange("p t d -> p (t d)"), PS[:, i, :], ACT.Exp,
                                         scale=-1.0).then_inc(act_eg, 1)
                if m is not None:
                    chunks(m, *C_BIAS)
                act.wait_ge(pe_mx, (b + 1) * TU + 1)
                with act.Fori(0, NG // 4) as i:
                    for u in (0, 2):
                        act.wait_ge(pe_eq2, b * NG + i * 4 + u + 1 + 1)
                        nc.scalar.activation(qET[:, bass.ds((i * 4 + u) * 2, 2), :],
                                             PSH[:, (2, 3, 0, 1)[u], :].rearrange("p (a s) -> p a s", a=2),
                                             ACT.Copy).then_inc(act_eq2, 1)
                with act.Fori(0, NG // 2) as i:
                    for u in range(2 * NU):
                        half, d = divmod(u, NU)
                        act.wait_ge(pe_sc, b * TU + i * 2 * NU + u + 1)
                        if d == 0:
                            act.wait_ge(pe_pv, b * NG + i * 2 + half + 1)
                        src = PS[:, 2 * (u % RING):2 * (u % RING) + 2, :].rearrange("p a c -> p (a c)")
                        if d < HG:
                            dst = PT[half][:, d, 0:1024]
                        else:
                            dst = PT[half][:, :, 1024:SW]
                            src = src.rearrange("p (h c) -> p h c", h=HG)
                        nc.scalar.activation(dst, src, ACT.Exp, scale=SCALE).then_inc(act_p, 1)
                for k in range(KT):
                    act.wait_ge(pe_aT, b * KT + k + 1)
                    nc.scalar.activation(aT[:, k, :], PS[:, 4 + k, :], ACT.Copy).then_inc(act_aT, 1)

            turn(0, None)
            with act.Fori(1, B - 1) as b:
                turn(b, b - 1)
            turn(B - 1, B - 2)
            m = B - 1
            x1T_parts(m)
            route(m)
            chunks(m, 0, 2)
            gate_rows(m)
            chunks(m, 2, NC)

        @block.gpsimd
        def _(pool):
            for credit in (pool_v, pool_e):
                pool.sem_inc(credit, 1)
            pool.sem_inc(pool_hp, 2)
            nc.gpsimd.memset(kz[1][:, :, :], 0.0).then_inc(s_one, 1)
            nc.gpsimd.memset(hp[:, :, :, :], 0.0)
            nc.gpsimd.memset(vst[:, :, :, :], 0.0)
            pool.drain()
            nc.gpsimd.memset(vst[:, :, :, HD:HD + 1], 1.0).then_inc(s_init, 1)
            pool.wait_ge(dve_w, 4)
            nc.gpsimd.memset(kz[0][:, :, :], 0.0).then_inc(s_init, 1)
            pool.drain()

            def low(m, c, slot):
                w = CHUNKS[c][1] if isinstance(c, int) else P
                pool.wait_ge(act_hp, m * NC + c + 1)
                nc.gpsimd.tensor_tensor(hp[0:w, slot, 1, :], hr[0:w, slot, :], hp[0:w, slot, 0, :],
                                        ALU.subtract).then_inc(pool_hp, 1)

            def turn(b, m):
                settled_wait(pool, pe_pv, b * NG + 2)
                nc.gpsimd.memset(EQ[:, :, :, CR:HW], 0.0)
                nc.gpsimd.memset(EK[:, :, :, CR + NCH:HW], 0.0)
                for j in range(NT):
                    nc.gpsimd.tensor_scalar(EK[:, j, :, CR:CR + NCH], ind[:, j:j + 1, :].to_broadcast([P, H, NCH]),
                                            1.0, 0.0, ALU.mult, ALU.add)
                    for n, (E, c0, hi, lo, step) in enumerate(((EQ, 0, 0, 2, 1), (EK, D, 0, 1, 2))):
                        pool.wait_ge(act_e, (b * NT + j) * 2 + n + 1)
                        src = rot[:, j, c0:c0 + D].rearrange("p (h d) -> p h d", h=H).unsqueeze(2).to_broadcast([P, H, 2, HD])
                        e4 = E[:, j, :, 0:CR].rearrange("p h (s d) -> p h s d", s=SLOTS)
                        ins = nc.gpsimd.tensor_tensor(e4[:, :, lo:lo + step + 1:step, :], src,
                                                      e4[:, :, hi:hi + step + 1:step, :], ALU.subtract)
                    ins.then_inc(pool_e, 1)
                if m is not None:
                    for c in range(*C_FIRST):
                        low(m, c, c % 2)
                    for (first, last), steps in ((C_TOPK, NG // 2), (C_MAX, MAX_STEPS)):
                        n = (last - first) // steps
                        pool.drain()
                        with pool.Fori(0, steps) as i:
                            for u in range(n):
                                low(m, i * n + first + u, (first + u) % 2)
                    for c in range(*C_BIAS):
                        low(m, c, c % 2)
                settled_wait(pool, act_v, (b + 1) * 2)
                with pool.Fori(0, NG) as g:
                    settled_wait(pool, pe_pv, b * NG + g + 2)
                    vg = v[:, :, bass.ds(g * HG * HD, HG * HD)].rearrange("p t (h d) -> p t h d", h=HG)
                    ones = vst[:, :, :, HD:HD + 1].to_broadcast([P, NT, HG, HD])
                    nc.gpsimd.tensor_tensor(vst[:, :, :, 0:HD], vg, ones, ALU.mult).then_inc(pool_v, 1)

            turn(0, None)
            with pool.Fori(1, B - 1) as b:
                turn(b, b - 1)
            turn(B - 1, B - 2)
            for c in range(NC):
                low(B - 1, c, c % 2)

        @block.vector
        def _(dve):
            for credit in (dve_x1, dve_z, dve_o, dve_otok, dve_h):
                dve.sem_inc(credit, 1)
            dve.sem_inc(dve_cm, RING)
            dve.sem_inc(dve_eq2, 2)
            dve.wait_ge(s_const, 16 * (NCONST - 1))
            nc.vector.memset(gmask[:, :, NCH:TOPW], PAD)
            nc.vector.memset(gext[:, :, NE:NE + NS], 1.0)
            nc.vector.memset(sc[:, :, NE:TOPW], PAD)
            nc.vector.tensor_tensor(rep[:, :, 0:NCH], gm_c[:, 0:1, :].to_broadcast([P, H, NCH]),
                                    sm_c[:, 0:1, :].to_broadcast([P, H, NCH]), ALU.max)
            dve.drain()
            nc.vector.tensor_scalar(cbias[:, 0], rep[:, :, 0:NCH], -OFF, None, ALU.max).then_inc(s_init, 1)
            for n in range(2):
                dve.wait_ge(act_w, n + 1)
                nc.vector.tensor_tensor(W1[:, 1, n, :], (UK, UQ)[n][:, 0:FS + FR], W1[:, 0, n, :], ALU.subtract).then_inc(dve_w, 1)
            for n, (c0, c1) in enumerate(((0, 13), (13, NC))):
                dve.wait_ge(act_w, n + 3)
                src = qf if n == 0 else kz[0][:, :, :].rearrange("p a s -> p (a s)").bitcast(F32)
                nc.vector.tensor_tensor(W2[:, 1, c0:c1, :].rearrange("p c n -> p (c n)"), src[:, 0:(c1 - c0) * D],
                                        W2[:, 0, c0:c1, :].rearrange("p c n -> p (c n)"), ALU.subtract).then_inc(dve_w, 1)
            dve.wait_ge(act_w, 5)
            nc.vector.tensor_tensor(CENT[:, 1], CENTF[:, :, :], CENT[:, 0], ALU.subtract).then_inc(dve_w, 1)
            nc.vector.tensor_scalar(WO[:, :, :], WO[:, :, :], onw, None, ALU.mult).then_inc(dve_w, 1)

            def link(ins):
                dve.drain()
                return ins

            def gated(m, c, slot):
                dve.wait_ge(pe_h, m * NC + c + 1)
                dve.wait_ge(act_h, m * NC + c + 2)
                nc.vector.tensor_tensor(hr[:, slot, :], hr[:, slot, :], PS[:, BK_G, :], ALU.mult).then_inc(dve_h, 1)

            def root(n):
                a, y, t = ms[:, 0:n], ry[:, 0:n], rt[:, 0:n]
                link(nc.vector.tensor_scalar(t.bitcast(I32), a.bitcast(I32), 1, None, ALU.logical_shift_right))
                link(nc.vector.tensor_scalar(y.bitcast(I32), t.bitcast(I32), -1.0, float(ROOT), ALU.mult, ALU.add))
                for _ in range(3):
                    link(nc.vector.tensor_tensor(t, y, y, ALU.mult))
                    link(nc.vector.scalar_tensor_tensor(out=t, in0=t, scalar=-0.5, in1=a, op0=ALU.mult, op1=ALU.mult))
                    link(nc.vector.scalar_tensor_tensor(out=y, in0=t, scalar=1.5, in1=y, op0=ALU.add, op1=ALU.mult))

            def layernorm(src, dst, done):
                for j in range(NT):
                    nc.vector.bn_stats(st6[:, j, :], src[:, j, :])
                dve.drain()
                for j in range(NT):
                    nc.vector.bn_aggr(mv[:, j, :], st6[:, j, :])
                dve.drain()
                link(nc.vector.tensor_scalar(ms[:, 0:NT], mv[:, :, 1], 1e-5, None, ALU.add))
                root(NT)
                for j in range(NT):
                    nc.vector.tensor_scalar(dst[:, j, :], src[:, j, :], mv[:, j, 0:1], ry[:, j:j + 1],
                                            ALU.subtract, ALU.mult).then_inc(done, 1)

            def x1T_parts(m):
                for k in range(KT):
                    dve.wait_ge(act_x1T, m * KT + k + 1)
                    nc.vector.tensor_tensor(x1T[:, 1, k, :], PS[:, 4 + k, :], x1T[:, 0, k, :], ALU.subtract).then_inc(dve_x1T, 1)

            def route(m):
                dve.wait_ge(act_rt, m + 1)
                link(nc.vector.tensor_scalar(er[:, :, :], er[:, :, :], 1.0, None, ALU.add))
                link(nc.vector.reciprocal(er[:, :, :], er[:, :, :]))
                link(nc.vector.tensor_tensor(sc[:, :, 0:NE], er[:, :, :], rbias.unsqueeze(1).to_broadcast([P, NT, NE]), ALU.add))
                for j in range(NT):
                    nc.vector.max(rtop[:, j, :], sc[:, j, 0:NE])
                dve.drain()
                link(nc.vector.memset(rtop[:, :, KR:8], PAD))
                for j in range(NT):
                    nc.vector.match_replace(rrep[:, j, :], rtop[:, j, :], sc[:, j, :], CHOSEN)
                dve.drain()
                link(nc.vector.scalar_tensor_tensor(out=gat[:, :, :], in0=rrep[:, :, 0:NE], scalar=BIG, in1=sc[:, :, 0:NE],
                                                    op0=ALU.is_gt, op1=ALU.mult))
                link(nc.vector.tensor_reduce(gsum[:, :], gat[:, :, :], AX.X, ALU.add))
                link(nc.vector.tensor_scalar(gsum[:, :], gsum[:, :], 1e-8, None, ALU.max))
                link(nc.vector.reciprocal(gsum[:, :], gsum[:, :]))
                gg = gext[:, :, 0:NE]
                link(nc.vector.tensor_tensor(gg, gat[:, :, :], gsum[:, :].unsqueeze(2).to_broadcast([P, NT, NE]), ALU.mult))
                link(nc.vector.tensor_copy(gsp[:, :, 0, :], gg))
                nc.vector.tensor_tensor(gsp[:, :, 1, :], gg, gsp[:, :, 0, :], ALU.subtract).then_inc(dve_g, 1)

            def finish(m):
                dve.wait_ge(pe_y, (m + 1) * NC + 2)
                for i in range(2):
                    xs = x1n[:, 2 * i:2 * i + 2, :].rearrange("p t d -> p (t d)")
                    nc.vector.scalar_tensor_tensor(out=xs, in0=xs, scalar=2.0, in1=PS[:, BK_Y + i, :],
                                                   op0=ALU.mult, op1=ALU.add).then_inc(dve_z, 1)
                dve.drain()
                layernorm(x1n, x1n, dve_out)
                dve.drain()

            def turn(b, m):
                if m is not None:
                    x1T_parts(m)
                for j in range(NT):
                    dve.wait_ge(pe_proj, b * NT + j + 1)
                    if j == 0:
                        dve.wait_ge(pe_pv, b * NG + 2)
                        dve.wait_ge(pe_oT, b * NG + 1)
                    t = PS[:, j, :].rearrange("p (h u f) -> p h u f", h=2 * H, u=2)
                    o = rot[:, j, :].rearrange("p (h u f) -> p h u f", h=2 * H, u=2)
                    w = ropeb[:, :].rearrange("p (h u f) -> p h u f", h=2 * H, u=2)
                    cj = cos[:, j:j + 1, :].to_broadcast([P, 2 * H, HD // 2])
                    sj = sin[:, j:j + 1, :].to_broadcast([P, 2 * H, HD // 2])
                    nc.vector.tensor_tensor(w[:, :, 0, :], t[:, :, 1, :], sj, ALU.mult)
                    nc.vector.tensor_tensor(w[:, :, 1, :], t[:, :, 0, :], sj, ALU.mult)
                    nc.vector.tensor_tensor(o[:, :, 0, :], t[:, :, 0, :], cj, ALU.mult)
                    link(nc.vector.tensor_tensor(o[:, :, 1, :], t[:, :, 1, :], cj, ALU.mult))
                    nc.vector.tensor_tensor(o[:, :, 0, :], o[:, :, 0, :], w[:, :, 0, :], ALU.subtract)
                    nc.vector.tensor_tensor(o[:, :, 1, :], o[:, :, 1, :], w[:, :, 1, :], ALU.add).then_inc(dve_rope, 1)
                    dve.drain()
                dve.wait_ge(pe_km, b + 1 + 1)
                for k in range(KT):
                    nc.vector.tensor_tensor(
                        KB[:, k, :].rearrange("p (h n) -> p h n", n=NCH),
                        PS[:, 2, k * NCH:(k + 1) * NCH].unsqueeze(1).to_broadcast([P, 16, NCH]),
                        bmask.unsqueeze(2).to_broadcast([P, 16, NCH]), ALU.mult).then_inc(dve_kb, 1)
                if m is not None:
                    route(m)
                c = C_TOPK[0]
                for j, bank in ((1, 3), (2, 0), (3, 1)):
                    dve.wait_ge(pe_gate, b * 3 + j + 1)
                    nc.vector.tensor_tensor(gmask[:, :, 0:NCH], PS[:, bank, :].rearrange("p (h n) -> p h n", n=NCH),
                                            gm_c[:, j:j + 1, :].to_broadcast([P, H, NCH]), ALU.add).then_inc(dve_gm, 1)
                    dve.drain()
                    for h in range(H):
                        nc.vector.max(top8[:, h, :], gmask[:, h, 0:NCH])
                    dve.drain()
                    if m is not None and j > 1:
                        gated(m, c, c % 2)
                        c += 1
                    link(nc.vector.memset(top8[:, :, TOPK - 1:8], PAD))
                    for q in range(4):
                        for h in range(8 * q, 8 * q + 8):
                            nc.vector.match_replace(rep[:, h, :], top8[:, h, :], gmask[:, h, :], CHOSEN)
                        if m is not None and j > 1 and q % 2:
                            gated(m, c, c % 2)
                            c += 1
                    dve.drain()
                    link(nc.vector.tensor_scalar(rep[:, :, 0:NCH], rep[:, :, 0:NCH], BIG, OFF, ALU.is_gt, ALU.mult))
                    link(nc.vector.tensor_tensor(rep[:, :, 0:NCH], rep[:, :, 0:NCH],
                                                 sm_c[:, j:j + 1, :].to_broadcast([P, H, NCH]), ALU.add))
                    link(nc.vector.tensor_scalar(cbias[:, j], rep[:, :, 0:NCH], -OFF, None, ALU.max))
                    if m is not None and j == 1:
                        gated(m, c, c % 2)
                        c += 1
                while m is not None and c < C_TOPK[1]:
                    gated(m, c, c % 2)
                    c += 1
                settled_wait(dve, pe_gate, (b + 1) * 3 + 1)
                with dve.Fori(0, MAX_STEPS) as i:
                    for u in range(MU):
                        dve.wait_ge(pe_mx, b * TU + i * MU + u + 1 + 1)
                        h0, d = (i * (NG // MAX_STEPS) + u // NU) * HG, u % NU
                        src = PS[:, 2 * (u % RING):2 * (u % RING) + 2, :].rearrange("p a (c k) -> p (a c) k", k=CHUNK)
                        if d < HG:
                            dst = CM[:, bass.ds(h0 + d, 1), 0:32].rearrange("p o c -> p (o c)")
                        else:
                            dst = CM[:, bass.ds(h0, HG), 32:40]
                            src = src.rearrange("p (h c) k -> p h c k", h=HG)
                        nc.vector.tensor_reduce(dst, src, AX.X, ALU.max).then_inc(dve_cm, 1)
                        for cc, part in dealt(u - 1) if m is not None and u else ():
                            if part == 3:
                                gated(m, i * MC + C_MAX[0] + cc, (C_MAX[0] + cc) % 2)
                dve.drain()
                for j in range(NT):
                    w = CPT * (j + 1)
                    link(nc.vector.scalar_tensor_tensor(out=rep[:, :, 0:w], in0=cbias[:, j, :, 0:w], scalar=UNIT,
                                                        in1=CM[:, :, MOFF[j] // CHUNK:MOFF[j] // CHUNK + w],
                                                        op0=ALU.mult, op1=ALU.add))
                    link(nc.vector.tensor_reduce(negm[:, :], rep[:, :, 0:w], AX.X, ALU.max, negate=True))
                    link(nc.vector.tensor_scalar(negm[:, :], negm[:, :], 1.0 / UNIT, None, ALU.mult))
                    if j == 0:
                        dve.wait_ge(pe_eq, (b + 1) * NG)
                    nc.vector.tensor_tensor(EQ[:, j, :, CR:CR + NCH], cbias[:, j],
                                            negm[:, :].unsqueeze(2).to_broadcast([P, H, NCH]), ALU.add).then_inc(dve_bias, 1)
                    dve.drain()
                    if m is not None and j % 2:
                        gated(m, C_BIAS[0] + j // 2, (C_BIAS[0] + j // 2) % 2)
                with dve.Fori(0, NG // 4) as i:
                    for u in (1, 3):
                        dve.wait_ge(pe_eq2, b * NG + i * 4 + u + 1 + 1)
                        nc.vector.tensor_copy(qET[:, bass.ds((i * 4 + u) * 2, 2), :],
                                              PSH[:, (2, 3, 0, 1)[u], :].rearrange("p (a s) -> p a s", a=2)).then_inc(dve_eq2, 1)
                if m is not None:
                    finish(m)
                dve.drain()
                settled_wait(dve, act_eg, (b + 1) * 2)
                e2 = eg.rearrange("p t d -> p (t d)")
                link(nc.vector.tensor_scalar(e2, e2, 1.0, None, ALU.add))
                with dve.Fori(0, NG) as g:
                    n = b * NG + g
                    dve.wait_ge(pe_pv, n + 1 + 2)
                    dve.wait_ge(pe_oT, n + 1)
                    nc.vector.tensor_copy(osb[:, :], PS[:, BK_PV, :]).then_inc(dve_o, 1)
                    w = NT * D // NG
                    nc.vector.reciprocal(e2[:, bass.ds(g * w, w)], e2[:, bass.ds(g * w, w)])
                    dve.wait_ge(pe_oT, n + 1 + 1)
                    nc.vector.tensor_copy(
                        otok.rearrange("p (t h) d -> p t h d", t=NT)[:, :, bass.ds(g * HG, HG), :],
                        PS[:, BK_OT, :].rearrange("p (t h d) -> p t h d", t=NT, h=HG)[:, :, :, 0:HD + 1]).then_inc(dve_otok, 1)
                dve.drain()
                u8, s1 = otok[:, :, 0:HD], otok[:, :, HD]
                link(nc.vector.tensor_tensor(sq, u8, u8, ALU.mult))
                link(nc.vector.tensor_reduce(ms[:, :], sq, AX.X, ALU.add))
                link(nc.vector.tensor_tensor(rt[:, :], s1, s1, ALU.mult))
                link(nc.vector.scalar_tensor_tensor(out=ms[:, :], in0=rt[:, :], scalar=HD * 1e-6, in1=ms[:, :],
                                                    op0=ALU.mult, op1=ALU.add))
                link(nc.vector.tensor_scalar(ms[:, :], ms[:, :], 1.0 / HD, None, ALU.mult))
                root(NT * H)
                link(nc.vector.tensor_tensor(u8, u8, ry[:, :].unsqueeze(2).to_broadcast([P, NT * H, HD]), ALU.mult))
                nc.vector.tensor_tensor(sq, u8, e2.rearrange("p (h d) -> p h d", d=HD), ALU.mult).then_inc(dve_on, 1)
                if m is not None:
                    settled_wait(dve, s_out, 16 * m + 32)
                dve.wait_ge(s_x, 16 * b + 16)
                for i in range(2):
                    dve.wait_ge(pe_att, 2 * b + i + 1)
                    nc.vector.tensor_tensor(x1n[:, 2 * i:2 * i + 2, :].rearrange("p t d -> p (t d)"), PS[:, 4 + i, :],
                                            x[:, 2 * i:2 * i + 2, :].rearrange("p t d -> p (t d)"), ALU.add).then_inc(dve_x1, 1)
                dve.drain()
                layernorm(x1n, x1n, dve_ln)

            turn(0, None)
            with dve.Fori(1, B - 1) as b:
                turn(b, b - 1)
            turn(B - 1, B - 2)
            m = B - 1
            x1T_parts(m)
            route(m)
            for c in range(NSH, NC):
                gated(m, c, c % 2)
            finish(m)


def kernel(**inputs):
    import numpy as np
    import ml_dtypes
    import concourse.bacc as bacc
    from concourse.bass_utils import run_bass_kernel_spmd as run

    a = {k[3:]: np.asarray(val) for k, val in inputs.items()}
    f32 = np.float32
    x = np.ascontiguousarray(a["attn_hidden_states"])
    cf = np.zeros((P, C_W), f32)
    p = np.arange(P)
    cf[:, C_ID:C_ID + P] = np.eye(P, dtype=f32)
    inv_freq = f32(1.0) / np.power(f32(10000.0), np.arange(0, HD, 2, dtype=f32) / f32(HD))
    freqs = np.arange(S, dtype=f32)[:, None] * inv_freq[None, :].astype(f32)
    tab = lambda t: t.astype(f32).reshape(NT, P, HD // 2).transpose(1, 0, 2).reshape(P, -1)
    cf[:, C_COS:C_COS + 16] = tab(np.cos(freqs))
    cf[:, C_SIN:C_SIN + 16] = tab(np.sin(freqs))
    cf[:, C_AVG:C_AVG + CPT] = (p[:, None] // CHUNK == np.arange(CPT)) / f32(CHUNK)
    cf[:, C_BM:C_BM + 16] = p[:, None] // HD == np.arange(16)
    own = (np.arange(NT)[None, :, None] * CPT + p[:, None, None] // CHUNK)
    n = np.arange(NCH)[None, None, :]
    cf[:, C_GM:C_GM + 64] = np.where(n < own, 0.0, -BIG).reshape(P, -1)
    cf[:, C_SM:C_SM + 64] = np.where(n == own, 0.0, -OFF).reshape(P, -1)
    ch = np.zeros((P, H_W), np.float16)
    ch[:, H_ID:H_ID + P] = np.eye(P)
    ch[:, H_IND:H_IND + 64] = np.where(n == own, UNIT, 0.0).reshape(P, -1)
    cg = np.zeros((P, G_W), f32)
    cg[:, G_ID:G_ID + P] = np.eye(P)
    cg[:, G_CQ:G_CQ + P] = np.where(p[None, :] > p[:, None], -BIG, 0.0)
    cg[:, G_CK:G_CK + P] = np.where(p[:, None] > p[None, :], -BIG, 0.0)
    one = np.tile((np.arange(FR) // DF)[None, :] == np.arange(NE)[:, None], (2, 1)).astype(np.float16)
    cf[:, C_ONW] = np.tile(a["attn_o_norm_weight"], P // HD)
    cf[:, C_RB:C_RB + NE] = a["ffn_bias"][None, :]
    b1 = np.concatenate([a["ffn_shared_b1"].reshape(-1), a["ffn_routed_b1"].reshape(-1)])
    w2f = np.concatenate([a["ffn_shared_w2"].reshape(-1, D), a["ffn_routed_w2"].reshape(-1, D)])
    w2 = np.zeros((NC * P, D), f32)
    for c, (f0, m) in enumerate(CHUNKS):
        cf[0:m, C_B1 + c] = b1[f0:f0 + m]
        w2[c * P:c * P + m] = w2f[f0:f0 + m]
    cols = lambda w: w.transpose(1, 0, 2).reshape(D, -1)
    arrays = {
        "in_xT": x.transpose(0, 2, 1),
        "in_x": x,
        "in_wa": np.concatenate([a["attn_Wq"].T, a["attn_Wk"].T, a["attn_Wv"].T, a["attn_Wg1"].T], axis=1),
        "in_wg2": a["attn_Wg2"].T,
        "in_wo": a["attn_Wo"].T,
        "in_w1": np.concatenate([cols(a["ffn_shared_w1"]), cols(a["ffn_routed_w1"])], axis=1),
        "in_w2": w2,
        "in_cent": a["ffn_centroids"].T,
        "in_b2": np.concatenate([a["ffn_routed_b2"], a["ffn_shared_b2"]]),
        "in_cf": cf,
        "in_ch": ch,
        "in_cg": cg.astype(ml_dtypes.bfloat16),
        "in_one": one,
    }
    arrays = {key: np.ascontiguousarray(val) for key, val in arrays.items()}
    nc = bacc.Bacc("TRN2", target_bir_lowering=False, num_devices=1)
    args = [nc.dram_tensor(key, val.shape, mybir.dt.from_np(val.dtype), kind="ExternalInput").ap()
            for key, val in arrays.items()]
    args.append(nc.dram_tensor("out", (B, S, D), F32, kind="ExternalOutput").ap())
    build(nc, *args)
    return run(nc, [arrays], core_ids=[0]).results[0]["out"]
```

```python
from contextlib import ExitStack

import concourse.bass as bass
from concourse import mybir
from concourse.alu_op_type import AluOpType as ALU

ACT = mybir.ActivationFunctionType
AX = mybir.AxisListType
F32 = mybir.dt.float32
F16 = mybir.dt.float16
BF16 = mybir.dt.bfloat16
I32 = mybir.dt.int32

P = 128
B, S, D = 8, 512, 256
H, HD = 32, 8
CHUNK, TOPK = 32, 4
NCH = S // CHUNK
NT = S // P
KT = D // P
CPT = P // CHUNK
KORDER = (0, 1, 3, 2)
HG = 4
NG = H // HG
SLOTS = 4
HW = 64
CR = SLOTS * HD
QW = D + D + D + HD
NE, NS, DF, KR = 16, 2, 176, 4
FS, FR = NS * DF, NE * DF
NSH = 3
CHUNKS = [(0, P), (P, P), (2 * P, FS - 2 * P)] + [(FS + P * i, P) for i in range(FR // P)]
NC = len(CHUNKS)
SCALE = HD ** -0.5
BIG = 1e30
PAD = -3e38
CHOSEN = 3e38
TOPW = NCH + 5
UNIT = 2.0 ** 15
OFF = 2.0 ** 15
ROOT = 0x5F3759DF
MOFF = {3: 0, 2: 512, 0: 896, 1: 1024}
POFF = {0: 0, 1: 512, 3: 896, 2: 1024}
SW = 1280
NU = 5
TU = NG * NU
RING = 2
PAIRS = ((0, 1, 0, 1, 0), (2, 1, 0, 2, 1), (0, 1, 2, 0, 1), (2, 0, 1, 2, 1))
BACK = ((2, 2, 2, 2, 2), (3, 3, 3, 3, 3), (3, 2, 4, 3, 3), (3, 3, 3, 3, 2))
C_FIRST, C_TOPK, C_MAX, C_BIAS = (0, 3), (3, 11), (11, 23), (23, 25)
MAX_STEPS = 2
MU = TU // MAX_STEPS
MC = (C_MAX[1] - C_MAX[0]) // MAX_STEPS
DEALT = [(c, part) for c in range(MC) for part in range(8)]


def dealt(u):
    return DEALT[u * len(DEALT) // MU:(u + 1) * len(DEALT) // MU]

C_ID, C_COS, C_SIN, C_AVG, C_BM, C_GM, C_SM, C_ONW, C_RB, C_B1 = 0, 128, 144, 160, 164, 180, 244, 308, 309, 325
C_W = C_B1 + NC
H_ID, H_IND, H_W = 0, 128, 192
G_ID, G_CQ, G_W = 0, 128, 256
ROW_G1 = 64
GP = 2 * NE + NS


def build(nc, xT_d, x_d, wa_d, wg2_d, wo_d, w1_d, w2_d, cent_d, b2_d, cf_d, ch_d, cg_d, one_d, out_d):
    with ExitStack() as ctx:
        def sb(name, shape, dt=F32):
            return ctx.enter_context(nc.sbuf_tensor(name, shape, dt))

        def sem(name):
            return ctx.enter_context(nc.semaphore(name))

        W1 = sb("W1", [P, 2, KT, FS + FR], F16)
        W2 = sb("W2", [P, 2, NC, D], F16)
        WA = sb("WA", [P, KT, QW])
        WO = sb("WO", [P, KT, D])
        CENT = sb("CENT", [P, 2, KT, NE], F16)
        ROWS = sb("ROWS", [P, FR], F16)
        WG2 = ROWS[ROW_G1:ROW_G1 + HD, 0:2 * D].bitcast(F32)
        onehot = ROWS[0:GP, :]
        CF = sb("CF", [P, C_W])
        CH = sb("CH", [P, H_W], F16)
        CG = sb("CG", [P, G_W], BF16)
        xT = sb("xT", [P, KT, S])
        UK = sb("UK", [P, 6144])
        UQ = sb("UQ", [P, HG * SW])
        EK = UK[:, 0:4096].bitcast(F16).rearrange("p (t h w) -> p t h w", t=NT, h=H)
        rot = UK[:, 4096:6144].rearrange("p (t c) -> p t c", t=NT)
        EQ = UQ[:, 0:4096].bitcast(F16).rearrange("p (t h w) -> p t h w", t=NT, h=H)
        PT = (UK[:, 0:HG * SW].rearrange("p (h w) -> p h w", h=HG),
              UQ[:, :].rearrange("p (h w) -> p h w", h=HG))
        ropeb = sb("ropeb", [P, 2 * D])
        KB = ropeb[:, :].rearrange("p (k d) -> p k d", k=KT)
        osb = ropeb
        v = sb("v", [P, NT, D])
        x = v
        qT = sb("qT", [P, KT, S])
        eg = qT[:, :, :].rearrange("p k s -> p (k s)").rearrange("p (t d) -> p t d", t=NT)
        gmask = sb("gmask", [P, H, TOPW])
        rep = sb("rep", [P, H, TOPW])
        cbias = sb("cbias", [P, NT, H, NCH], F16)
        qET = sb("qET", [P, H // 2, S], F16)
        qf = qET[:, :, :].rearrange("p a s -> p (a s)").bitcast(F32)
        aT = qf[:, 0:1024].rearrange("p (k s) -> p k s", k=KT)
        kz = (sb("kz0", [P, H // 2, S], F16),
              sb("kz1", [P, H // 2, S], F16))
        CM = sb("CM", [P, H, SW // CHUNK])
        cmf = CM[:, :, :].rearrange("p h c -> p (h c)")
        top8 = cmf[:, 0:H * 8].rearrange("p (h e) -> p h e", h=H)
        otok = cmf[:, 0:NT * 2 * HG * (HD + 1)].rearrange("p (t h d) -> p t h d", t=NT, h=2 * HG)
        sq = cmf[:, 512:512 + NT * 2 * HG * HD].rearrange("p (t h d) -> p t h d", t=NT, h=2 * HG)
        vst = sb("vst", [P, 2, NT, HG, HD + 1])
        repf = rep[:, :, :].rearrange("p h w -> p (h w)")
        ms, ry, rt = (repf[:, n * NT * H:(n + 1) * NT * H] for n in range(3))
        st6 = repf[:, 3 * NT * H:3 * NT * H + NT * 6].rearrange("p (t s) -> p t s", t=NT)
        mv = repf[:, 3 * NT * H + NT * 6:3 * NT * H + NT * 8].rearrange("p (t s) -> p t s", t=NT)
        x1n = sb("x1n", [P, NT, D])
        x1T = sb("x1T", [P, 2, KT, S], F16)
        er = sb("er", [P, NT, NE])
        CENTF = er[:, 0:KT, :]
        sc = sb("sc", [P, NT, TOPW])
        rtop = sb("rtop", [P, NT, 8])
        rrep = sb("rrep", [P, NT, TOPW])
        gat = er
        negm = rtop[:, :, :].rearrange("p t e -> p (t e)")
        gsum = sb("gsum", [P, NT])
        gsp = sb("gsp", [P, NT, GP], F16)
        GR = sb("GR", [P, S])
        g1T = GR[ROW_G1:ROW_G1 + HD, :]
        gTp = GR[0:GP, 0:S // 2].bitcast(F16)
        B2 = GR[0:GP, S // 2:S].bitcast(F16).rearrange("p (e d) -> p e d", e=2)
        hr = sb("hr", [P, 2, S])
        B2F = hr[0:GP, 0, 0:D]
        hp = sb("hp", [P, 2, 2, S], F16)

        PS = ctx.enter_context(nc.psum_tensor("PS", [P, 8, 512], F32))
        PSH = PS[:, :, :].bitcast(F16)
        BK_H, BK_G, BK_Y = 4, 5, 6
        BK_PV, BK_OT = 4, 5

        ident = CF[:, C_ID:C_ID + P]
        cos = CF[:, C_COS:C_COS + 16].rearrange("p (t f) -> p t f", t=NT)
        sin = CF[:, C_SIN:C_SIN + 16].rearrange("p (t f) -> p t f", t=NT)
        avg = CF[:, C_AVG:C_AVG + CPT]
        bmask = CF[:, C_BM:C_BM + 16]
        gm_c = CF[:, C_GM:C_GM + 64].rearrange("p (t n) -> p t n", t=NT)
        sm_c = CF[:, C_SM:C_SM + 64].rearrange("p (t n) -> p t n", t=NT)
        onw = CF[:, C_ONW:C_ONW + 1]
        rbias = CF[:, C_RB:C_RB + NE]
        b1 = CF[:, C_B1:C_B1 + NC]
        identh = CH[:, H_ID:H_ID + P]
        ind = CH[:, H_IND:H_IND + 64].rearrange("p (t n) -> p t n", t=NT)
        identb = CG[:, G_ID:G_ID + P]
        causal_q = CG[:, G_CQ:G_CQ + P]

        s_const = sem("s_const")
        s_small = sem("s_small")
        s_w = [sem(f"s_w{n}") for n in range(4)]
        s_init = sem("s_init")
        s_one = sem("s_one")
        act_w = sem("act_w")
        dve_w = sem("dve_w")
        s_xT = sem("s_xT")
        s_x = sem("s_x")
        s_out = sem("s_out")
        pe_proj = sem("pe_proj")
        dve_rope = sem("dve_rope")
        act_v = sem("act_v")
        act_e = sem("act_e")
        pool_e = sem("pool_e")
        pe_qT = sem("pe_qT")
        act_qT = sem("act_qT")
        pe_km = sem("pe_km")
        dve_kb = sem("dve_kb")
        pe_gate = sem("pe_gate")
        dve_gm = sem("dve_gm")
        pe_ek = sem("pe_ek")
        act_kz = sem("act_kz")
        pe_eq = sem("pe_eq")
        act_eq = sem("act_eq")
        pe_mx = sem("pe_mx")
        dve_cm = sem("dve_cm")
        dve_bias = sem("dve_bias")
        pe_eq2 = sem("pe_eq2")
        act_eq2 = sem("act_eq2")
        pe_g1 = sem("pe_g1")
        act_g1 = sem("act_g1")
        pe_g = sem("pe_g")
        act_eg = sem("act_eg")
        pe_sc = sem("pe_sc")
        act_p = sem("act_p")
        pool_v = sem("pool_v")
        pool_p = sem("pool_p")
        pe_pv = sem("pe_pv")
        dve_o = sem("dve_o")
        pe_oT = sem("pe_oT")
        dve_otok = sem("dve_otok")
        dve_on = sem("dve_on")
        pe_aT = sem("pe_aT")
        act_aT = sem("act_aT")
        pe_att = sem("pe_att")
        dve_x1 = sem("dve_x1")
        dve_ln = sem("dve_ln")
        pe_x1T = sem("pe_x1T")
        act_x1T = sem("act_x1T")
        dve_x1T = sem("dve_x1T")
        pe_rt = sem("pe_rt")
        act_rt = sem("act_rt")
        dve_g = sem("dve_g")
        pe_gT = sem("pe_gT")
        act_gT = sem("act_gT")
        pe_h = sem("pe_h")
        act_h = sem("act_h")
        dve_h = sem("dve_h")
        s_high = sem("s_high")
        pool_hp = sem("pool_hp")
        pe_y = sem("pe_y")
        dve_z = sem("dve_z")
        dve_out = sem("dve_out")

        def settled_wait(eng, which, count):
            if not isinstance(count, int):
                count = eng.to_reg(count)
                eng.wait_ge(s_one, 1)
            eng.wait_ge(which, count)

        block = ctx.enter_context(nc.Block())
        N_CONST, N_SMALL = 4, 5

        @block.sync
        def _(sp):
            sp.sem_inc(s_out, 16)
            sp.dma_start(xT[:, :, :], xT_d[0:1].rearrange("o (k p) s -> p (o k) s", p=P)).then_inc(s_xT, 16)
            for dst, src in ((WA[:, :, :], wa_d.rearrange("(k p) n -> p k n", p=P)),
                             (CF[:, :], cf_d), (CH[:, :], ch_d), (CG[:, :], cg_d)):
                sp.dma_start(dst, src).then_inc(s_const, 16)
            w1_v = w1_d.rearrange("(k p) n -> k p n", p=P)
            w2_v = w2_d.rearrange("(c p) n -> p c n", p=P)
            k0f = kz[0][:, :, :].rearrange("p a s -> p (a s)").bitcast(F32)
            sp.dma_start(UK[:, 0:FS + FR], w1_v[0]).then_inc(s_w[0], 16)
            sp.dma_start(UQ[:, 0:FS + FR], w1_v[1]).then_inc(s_w[1], 16)
            for dst, src in ((WG2, wg2_d), (B2F, b2_d), (onehot, one_d),
                             (WO[:, :, :], wo_d.rearrange("(k p) n -> p k n", p=P)),
                             (CENTF[:, :, :], cent_d.rearrange("(k p) n -> p k n", p=P))):
                sp.dma_start(dst, src).then_inc(s_small, 16)
            sp.dma_start(qf[:, 0:13 * D].rearrange("p (c n) -> p c n", n=D), w2_v[:, 0:13]).then_inc(s_w[2], 16)
            sp.dma_start(k0f[:, 0:12 * D].rearrange("p (c n) -> p c n", n=D), w2_v[:, 13:NC]).then_inc(s_w[3], 16)

            def load_xT(b):
                sp.dma_start(xT[:, :, :], xT_d[bass.ds(b, 1)].rearrange("o (k p) s -> p (o k) s", p=P)).then_inc(s_xT, 16)

            def load_x(b):
                settled_wait(sp, pool_v, (b + 1) * NG + 1)
                sp.dma_start(x[:, :, :], x_d[bass.ds(b, 1)].rearrange("o (t p) d -> p (o t) d", p=P)).then_inc(s_x, 16)

            def store(b):
                settled_wait(sp, dve_out, (b + 1) * NT)
                sp.dma_start(out_d[bass.ds(b, 1)].rearrange("o (t p) d -> p (o t) d", p=P), x1n[:, :, :]).then_inc(s_out, 16)

            sp.wait_ge(pe_g1, 1)
            load_xT(1)
            load_x(0)
            with sp.Fori(1, B - 1) as b:
                settled_wait(sp, pe_g1, b + 1)
                load_xT(b + 1)
                store(b - 1)
                load_x(b)
            store(B - 2)
            load_x(B - 1)
            store(B - 1)
            sp.wait_ge(s_out, 16 * B + 16)

        @block.tensor
        def _(pe):
            for credit in (pe_km, pe_gate, pe_mx, pe_oT):
                pe.sem_inc(credit, 1)
            pe.sem_inc(pe_y, 2)
            pe.sem_inc(pe_pv, 2)
            pe.wait_ge(s_const, 16 * N_CONST)

            def project_v(b, j):
                if j == 0:
                    pe.wait_ge(s_xT, 16 * b + 16)
                for k in range(KT):
                    pe.matmul(PS[:, BK_Y + j // 2, (j % 2) * D:(j % 2 + 1) * D], xT[:, k, j * P:(j + 1) * P],
                              WA[:, k, 2 * D:3 * D], start=(k == 0), stop=(k == KT - 1))

            def project_qk(b, j):
                for k in range(KT):
                    mm = pe.matmul(PS[:, j, :], xT[:, k, j * P:(j + 1) * P], WA[:, k, 0:2 * D],
                                   start=(k == 0), stop=(k == KT - 1))
                mm.then_inc(pe_proj, 1)

            def project(b, first, last):
                for j in range(first, last):
                    project_v(b, j)
                    project_qk(b, j)

            def rank_rows(b):
                pe.wait_ge(act_v, 2 * b + 2)
                for k in range(KT):
                    mm = pe.matmul(PS[ROW_G1:ROW_G1 + HD, BK_Y, :], WA[:, k, 3 * D:QW], xT[:, k, :], start=(k == 0),
                                   stop=(k == KT - 1), tile_position=(0, ROW_G1))
                mm.then_inc(pe_g1, 1)

            def transpose_q(b, first, last):
                for m in range(KT):
                    for j in range(first, last):
                        mm = pe.transpose(PS[:, m, j * P:(j + 1) * P], rot[:, j, m * P:(m + 1) * P], ident)
                    if last == NT:
                        mm.then_inc(pe_qT, 1)

            def chunk_means(b, first, last):
                for j in range(first, last):
                    for m in range(KT):
                        mm = pe.matmul(PS[:, BK_Y + 1, D + m * NCH + j * CPT:D + m * NCH + (j + 1) * CPT],
                                       rot[:, j, D + m * P:D + (m + 1) * P], avg, start=True, stop=True)
                if last == NT:
                    mm.then_inc(pe_km, 1)

            def chunk_gates(b):
                pe.wait_ge(act_qT, (b + 1) * KT)
                pe.wait_ge(dve_kb, (b + 1) * KT)
                for j, bank in ((1, 3), (2, 0), (3, 1)):
                    for m in range(KT):
                        mm = pe.matmul(PS[:, bank, m * D:(m + 1) * D], qT[:, m, j * P:(j + 1) * P], KB[:, m, :],
                                       start=True, stop=True)
                    mm.then_inc(pe_gate, 1)

            def stack(E, bank, g, done):
                for j in range(NT):
                    for pr in range(2):
                        mm = pe.transpose(PSH[:, bank, pr * S + j * P:pr * S + (j + 1) * P],
                                          E[:, j, bass.ds(g * HG + 2 * pr, 2), :].rearrange("p h w -> p (h w)"), identh)
                mm.then_inc(done, 1)

            def score_unit(g, r, d, by_key):
                r = (0, 2, BK_Y)[r]
                flat = PS[:, r:r + 2, :].rearrange("p a c -> p (a c)")
                off, wide = (POFF, (0, 1, 3)) if by_key else (MOFF, (3, 2, 0))
                narrow = 2 if by_key else 1
                blocks = [(d, t, off[t]) for t in wide] if d < HG else [(h, narrow, h * 256) for h in range(HG)]
                for h, t, o in blocks:
                    pair = bass.ds(g * 2 + h // 2, 1)
                    if by_key:
                        w = S - P * t
                        lhsT, rhs = kz[h % 2][:, pair, t * P:(t + 1) * P], qET[:, pair, t * P:S]
                    else:
                        w, diag = P * (t + 1), o + P * t
                        lhsT, rhs = qET[:, pair, t * P:(t + 1) * P], kz[h % 2][:, pair, 0:w]
                    mm = pe.matmul(flat[:, o:o + w], lhsT.rearrange("p o s -> p (o s)"), rhs.rearrange("p o s -> p (o s)"),
                                   start=True, stop=by_key)
                    if not by_key:
                        mm = pe.matmul(flat[:, diag:diag + P], identb, causal_q, start=False, stop=True)
                mm.then_inc(pe_sc if by_key else pe_mx, 1)

            def x1_transpose(m):
                pe.wait_ge(dve_ln, (m + 1) * NT)
                for k in range(KT):
                    for j in range(NT):
                        mm = pe.transpose(PS[:, 4 + k, j * P:(j + 1) * P], x1n[:, j, k * P:(k + 1) * P], ident)
                    mm.then_inc(pe_x1T, 1)

            def router(m):
                pe.wait_ge(dve_z, 2 * m + 1)
                pe.wait_ge(act_x1T, (m + 1) * KT)
                pe.wait_ge(dve_x1T, (m + 1) * KT)
                pe.wait_ge(act_g1, min(m + 2, B) if isinstance(m, int) else m + 2)
                for j in range(NT):
                    for n, (k, a, c) in enumerate((k, a, c) for k in range(KT) for a, c in ((0, 0), (0, 1), (1, 0))):
                        mm = pe.matmul(PS[:, BK_Y, j * NE:(j + 1) * NE], x1T[:, a, k, j * P:(j + 1) * P], CENT[:, c, k, :],
                                       start=(n == 0), stop=(n == 3 * KT - 1))
                mm.then_inc(pe_rt, 1)

            def gate_rows(m):
                settled_wait(pe, dve_g, m + 1)
                for j in range(NT):
                    mm = pe.transpose(PSH[0:GP, BK_Y + 1, j * P:(j + 1) * P], gsp[:, j, :], identh)
                mm.then_inc(pe_gT, 1)

            def open_outputs(m):
                pe.wait_ge(act_gT, m + 1)
                for j in range(NT):
                    for e in range(2):
                        pe.matmul(PS[:, BK_Y + j // 2, (j % 2) * D:(j % 2 + 1) * D], gTp[:, j * P:(j + 1) * P], B2[:, e, :],
                                  start=(j % 2 == 0 and e == 0), stop=False, skip_group_check=True)

            def hidden_cols(c):
                return CHUNKS[c] if isinstance(c, int) else (FS + (c - NSH) * P, P)

            def up(m, c, part):
                f0, w = hidden_cols(c)
                if part == 0:
                    pe.wait_ge(act_h, m * NC + c + 1)
                for n in (2 * part, 2 * part + 1):
                    k, (a, e) = n // 3, ((0, 0), (0, 1), (1, 0))[n % 3]
                    mm = pe.matmul(PS[0:w, BK_H, :], W1[:, a, k, bass.ds(f0, w)], x1T[:, e, k, :],
                                   start=(n == 0), stop=(n == 5))
                if part == 2 and isinstance(c, int) and c < NSH:
                    mm.then_inc(pe_h, 1)

            def gate_of(m, c):
                pe.wait_ge(dve_h, m * (NC - NSH) + c - NSH + 1)
                pe.matmul(PS[:, BK_G, :], onehot[:, bass.ds((c - NSH) * P, P)], gTp, start=True, stop=True).then_inc(pe_h, 1)

            def down(m, c, slot, j):
                w = hidden_cols(c)[1]
                if j == 0:
                    pe.wait_ge(pool_hp, m * NC + c + 3)
                for a, e in ((0, 0), (0, 1), (1, 0)):
                    last = isinstance(c, int) and c == NC - 1 and (a, e) == (1, 0)
                    mm = pe.matmul(PS[:, BK_Y + j // 2, (j % 2) * D:(j % 2 + 1) * D], hp[0:w, slot, a, j * P:(j + 1) * P],
                                   W2[0:w, e, bass.ds(c, 1), :].rearrange("p o n -> p (o n)"), start=False, stop=last,
                                   skip_group_check=True)
                if j == NT - 1:
                    mm.then_inc(pe_y, 1)

            def turn(b, m, more):
                rank_rows(b)
                pe.wait_ge(dve_rope, b * NT + 2)
                transpose_q(b, 0, 2)
                chunk_means(b, 0, 2)
                if m is not None:
                    x1_transpose(m)
                    router(m)
                    up(m, 0, 0)
                pe.wait_ge(dve_rope, (b + 1) * NT)
                chunk_means(b, 2, NT)
                transpose_q(b, 2, NT)
                if m is not None:
                    up(m, 0, 1)
                    up(m, 0, 2)
                chunk_gates(b)
                if m is not None:
                    gate_rows(m)
                    for part in range(3):
                        up(m, 1, part)
                    open_outputs(m)
                    for j in range(NT):
                        down(m, 0, 0, j)
                    for part in range(3):
                        up(m, 2, part)
                    for j in range(NT):
                        down(m, 1, 1, j)
                if m is None:
                    pe.wait_ge(act_w, 6)
                    pe.wait_ge(dve_w, 7)
                pe.wait_ge(act_g1, b + 1)
                settled_wait(pe, dve_gm, b * 3 + 1)
                with pe.Fori(0, NG // 2) as i:
                    for u in range(2):
                        n = b * NG + i * 2 + u
                        if m is not None:
                            c = i * 2 + C_TOPK[0] + u
                            for part in range(3):
                                up(m, c, part)
                            gate_of(m, c)
                        if u == 0:
                            pe.wait_ge(pool_e, (b + 1) * NT + 1)
                        pe.wait_ge(act_kz, 2 * n + 1)
                        stack(EK, 2, i * 2 + u, pe_ek)
                        pe.wait_ge(act_eq, n + 1)
                        stack(EQ, 3, i * 2 + u, pe_eq)
                        if m is not None:
                            for j in range(NT):
                                down(m, c - 1, (C_TOPK[0] + u - 1) % 2, j)
                if m is None:
                    pe.wait_ge(s_init, 3)
                settled_wait(pe, dve_gm, (b + 1) * 3)
                with pe.Fori(0, MAX_STEPS) as i:
                    for u in range(MU):
                        if u == 1:
                            pe.wait_ge(act_kz, (b + 1) * 2 * NG + 1)
                            pe.wait_ge(act_eq, (b + 1) * NG + 1)
                        pe.wait_ge(dve_cm, b * TU + i * MU + u + 1)
                        score_unit(i * (NG // MAX_STEPS) + u // NU, u % RING, u % NU, False)
                        for cc, part in dealt(u) if m is not None else ():
                            c = i * MC + C_MAX[0] + cc
                            if part < 3:
                                up(m, c, part)
                            elif part == 3:
                                gate_of(m, c)
                            else:
                                down(m, c - 1, (C_MAX[0] + cc - 1) % 2, part - 4)
                if m is not None:
                    for part in range(3):
                        up(m, NC - 2, part)
                pe.wait_ge(dve_cm, (b + 1) * TU + RING)
                for j in range(NT):
                    mm = pe.matmul(PS[:, j // 2, (j % 2) * D:(j % 2 + 1) * D], g1T[:, j * P:(j + 1) * P], WG2,
                                   start=True, stop=True, tile_position=(ROW_G1, 0))
                    if j % 2:
                        mm.then_inc(pe_g, 1)
                def restack(j):
                    settled_wait(pe, dve_bias, b * NT + j + 1)
                    if j >= 2:
                        pe.wait_ge(act_eq2, b * 2 * NT + 2 * (j - 1))
                    elif j == 1:
                        pe.wait_ge(act_eg, 2 * b + 2)
                    for n in range(2):
                        for pr in range(8):
                            mm = pe.transpose(PSH[:, (2, 0)[j % 2] + n, pr * P:(pr + 1) * P],
                                              EQ[:, j, 16 * n + 2 * pr:16 * n + 2 * pr + 2, :].rearrange("p h w -> p (h w)"), identh)
                        mm.then_inc(pe_eq2, 1)

                def late_down(c):
                    for j in range(NT):
                        down(m, c, c % 2, j)

                if m is not None:
                    gate_of(m, NC - 2)
                restack(0)
                if m is not None:
                    late_down(NC - 3)
                    for part in range(3):
                        up(m, NC - 1, part)
                restack(1)
                if m is not None:
                    gate_of(m, NC - 1)
                restack(2)
                restack(3)
                if m is not None:
                    late_down(NC - 2)
                    late_down(NC - 1)
                settled_wait(pe, act_eq2, (b + 1) * 2 * NT)

                def unit(g, gs, d):
                    pe.wait_ge(act_p, b * TU + g * NU + d + 1 + RING - BACK[gs][d])
                    if gs == 1 and d == 0 and m is not None:
                        pe.wait_ge(dve_z, 2 * m + 3)
                    score_unit(g, PAIRS[gs][d], d, True)

                def outputs(g, gs, n):
                    t = KORDER[n]
                    pe.wait_ge(pool_p, (b * NG + g) * NT + n + 1)
                    if n == 0:
                        pe.wait_ge(pool_v, b * NG + g + 1 + 1)
                        pe.wait_ge(dve_o, b * NG + g + 1)
                    o, w = POFF[t], S - P * t
                    for hh in range(HG):
                        mm = pe.matmul(PS[32 * hh:32 * hh + HD + 1, BK_PV, t * P:S], vst[:, gs % 2, t, hh, :], PT[gs % 2][:, hh, o:o + w],
                                       start=(n == 0), stop=(n == NT - 1), skip_group_check=True, tile_position=(0, 32 * hh))
                    if n == NT - 1:
                        mm.then_inc(pe_pv, 1)

                def to_tokens(g):
                    n = b * NG + g
                    pe.wait_ge(dve_o, n + 1 + 1)
                    pe.wait_ge(dve_otok, n + 1)
                    for j in range(NT):
                        mm = pe.transpose(PS[:, BK_OT, j * P:(j + 1) * P], osb[:, j * P:(j + 1) * P], ident)
                    mm.then_inc(pe_oT, 1)

                def group(g, gs):
                    for d in range(3):
                        unit(g, gs, d)
                    if gs > 1:
                        to_tokens(g - 2)
                    for t in range(NT):
                        outputs(g - 1, gs - 1, t)
                        if t + 3 < NU:
                            unit(g, gs, t + 3)

                for d in range(NU):
                    unit(0, 0, d)
                group(1, 1)
                with pe.Fori(0, NG // 2 - 1) as i:
                    for u in range(2):
                        group(i * 2 + 2 + u, 2 + u)
                if more:
                    pe.wait_ge(act_p, (b + 1) * TU + RING - 1)
                    project_v(b + 1, 0)
                to_tokens(NG - 2)
                for t in range(NT):
                    outputs(NG - 1, NG - 1, t)
                if more:
                    pe.wait_ge(act_p, (b + 1) * TU + RING)
                    project_qk(b + 1, 0)
                to_tokens(NG - 1)
                if more:
                    project(b + 1, 1, NT - 1)
                pe.wait_ge(dve_on, (b + 1) * (NG // 2))
                for k in range(KT):
                    for j in range(NT):
                        mm = pe.transpose(PS[:, 4 + k, j * P:(j + 1) * P], eg[:, j, k * P:(k + 1) * P], ident)
                    mm.then_inc(pe_aT, 1)
                pe.wait_ge(act_aT, (b + 1) * KT)
                for j in range(NT):
                    for k in range(KT):
                        mm = pe.matmul(PS[:, 4 + j // 2, (j % 2) * D:(j % 2 + 1) * D], aT[:, k, j * P:(j + 1) * P],
                                       WO[:, k, :], start=(k == 0), stop=(k == KT - 1))
                    if j % 2:
                        mm.then_inc(pe_att, 1)
                if more:
                    project(b + 1, NT - 1, NT)

            project(0, 0, NT)
            turn(0, None, True)
            with pe.Fori(1, B - 1) as b:
                turn(b, b - 1, True)
            turn(B - 1, B - 2, False)
            m = B - 1
            x1_transpose(m)
            router(m)
            for c in (0, 1):
                for part in range(3):
                    up(m, c, part)
            gate_rows(m)
            open_outputs(m)
            for c in range(2, NC + 2):
                if c < NC:
                    for part in range(3):
                        up(m, c, part)
                    if c >= NSH:
                        gate_of(m, c)
                for j in range(NT):
                    down(m, c - 2, c % 2, j)

        @block.scalar
        def _(act):
            for credit in (act_kz, act_eq, act_h):
                act.sem_inc(credit, 1)
            act.wait_ge(s_const, 16 * N_CONST)
            nc.scalar.activation(hr[:, 1, 0:1], CF[:, 0:1], ACT.Exp).then_inc(act_p, RING)
            for n in range(2):
                act.wait_ge(s_w[n], 16)
                nc.scalar.activation(W1[:, 0, n, :], (UK, UQ)[n][:, 0:FS + FR], ACT.Copy).then_inc(act_w, 1)

            def high_w2(n):
                c0, c1 = ((0, 13), (13, NC))[n]
                act.wait_ge(s_w[n + 2], 16)
                src = qf if n == 0 else kz[0][:, :, :].rearrange("p a s -> p (a s)").bitcast(F32)
                nc.scalar.activation(W2[:, 0, c0:c1, :].rearrange("p c n -> p (c n)"), src[:, 0:(c1 - c0) * D],
                                     ACT.Copy).then_inc(act_w, 1)

            def relu(m, c, slot):
                w = CHUNKS[c][1] if isinstance(c, int) else P
                act.wait_ge(pe_h, m * NC + c + 1)
                act.wait_ge(pool_hp, m * NC + c + 1)
                bias = b1[0:w, c:c + 1] if isinstance(c, int) else b1[:, bass.ds(c, 1)]
                nc.scalar.activation(hr[0:w, slot, :], PS[0:w, BK_H, :], ACT.Relu, bias=bias).then_inc(act_h, 1)

            def high(m, c, slot):
                w = CHUNKS[c][1] if isinstance(c, int) else P
                if isinstance(c, int) and c < NSH:
                    act.wait_ge(act_h, m * NC + c + 2)
                else:
                    act.wait_ge(dve_h, m * (NC - NSH) + c - NSH + 2)
                act.wait_ge(pe_y, m * NC + c + 1)
                nc.scalar.activation(hp[0:w, slot, 0, :], hr[0:w, slot, :], ACT.Copy).then_inc(s_high, 1)

            def chunks(m, first, last):
                for c in range(first, last):
                    relu(m, c, c % 2)
                    high(m, c, c % 2)

            def x1T_parts(m):
                for k in range(KT):
                    act.wait_ge(pe_x1T, m * KT + k + 1)
                    if k == 0:
                        act.wait_ge(pe_y, m * NC + 2)
                    nc.scalar.activation(x1T[:, 0, k, :], PS[:, 4 + k, :], ACT.Copy).then_inc(act_x1T, 1)

            def route(m):
                act.wait_ge(pe_rt, m + 1)
                nc.scalar.activation(er[:, :, :].rearrange("p t e -> p (t e)"), PS[:, BK_Y, 0:NT * NE], ACT.Exp,
                                     scale=-1.0).then_inc(act_rt, 1)

            def gate_rows(m):
                act.wait_ge(pe_gT, m + 1)
                nc.scalar.activation(gTp, PSH[0:GP, BK_Y + 1, 0:S], ACT.Copy).then_inc(act_gT, 1)

            def stack_high(b, first, last):
                for j in range(first, last):
                    act.wait_ge(dve_rope, b * NT + j + 1)
                    if j == 0:
                        act.wait_ge(pe_pv, b * NG + 2)
                    for E, c0, s0, step in ((EQ, 0, 0, 1), (EK, D, 0, 2)):
                        src = rot[:, j, c0:c0 + D].rearrange("p (h d) -> p h d", h=H).unsqueeze(2).to_broadcast([P, H, 2, HD])
                        dst = E[:, j, :, 0:CR].rearrange("p h (s d) -> p h s d", s=SLOTS)[:, :, s0:s0 + step + 1:step, :]
                        nc.scalar.activation(dst, src, ACT.Copy).then_inc(act_e, 1)

            def copy_v(b):
                for i in range(2):
                    act.wait_ge(pe_proj, b * NT + 2 * i + 2)
                    if i == 0:
                        act.wait_ge(dve_x1, 2 * b + 1)
                    nc.scalar.activation(v[:, 2 * i:2 * i + 2, :].rearrange("p t d -> p (t d)"), PS[:, BK_Y + i, :],
                                         ACT.Copy).then_inc(act_v, 1)

            def turn(b, m, more):
                act.wait_ge(pe_g1, b + 1)
                nc.scalar.activation(g1T, PS[ROW_G1:ROW_G1 + HD, BK_Y, :], ACT.Copy).then_inc(act_g1, 1)
                if m is not None:
                    x1T_parts(m)
                stack_high(b, 2, 3)
                if m is not None:
                    route(m)
                for k in range(KT):
                    act.wait_ge(pe_qT, b * KT + k + 1)
                    nc.scalar.activation(qT[:, k, :], PS[:, k, :], ACT.Copy).then_inc(act_qT, 1)
                stack_high(b, 3, NT)
                if m is not None:
                    chunks(m, 0, 1)
                if m is not None:
                    gate_rows(m)
                    chunks(m, 1, C_FIRST[1])
                with act.Fori(0, NG // 2) as i:
                    for u in range(2):
                        n = b * NG + i * 2 + u
                        if m is not None:
                            c = i * 2 + C_TOPK[0] + u
                            relu(m, c, (C_TOPK[0] + u) % 2)
                        act.wait_ge(pe_ek, n + 1)
                        for h in range(2):
                            nc.scalar.activation(kz[h][64 * h:64 * h + 64, bass.ds(i * 4 + u * 2, 2), :],
                                                 PSH[64 * h:64 * h + 64, 2, :].rearrange("p (a s) -> p a s", a=2),
                                                 ACT.Copy).then_inc(act_kz, 1)
                        act.wait_ge(pe_eq, n + 1)
                        nc.scalar.activation(qET[:, bass.ds(i * 4 + u * 2, 2), :],
                                             PSH[:, 3, :].rearrange("p (a s) -> p a s", a=2), ACT.Copy).then_inc(act_eq, 1)
                if m is not None:
                    with act.Fori(0, MAX_STEPS) as i:
                        for u in range(MC):
                            c = i * MC + C_MAX[0] + u
                            relu(m, c, (C_MAX[0] + u) % 2)
                            high(m, c, (C_MAX[0] + u) % 2)
                for i in range(2):
                    act.wait_ge(pe_g, 2 * b + i + 1)
                    nc.scalar.activation(eg[:, 2 * i:2 * i + 2, :].rearrange("p t d -> p (t d)"), PS[:, i, :], ACT.Exp,
                                         scale=-1.0).then_inc(act_eg, 1)
                act.wait_ge(pe_mx, (b + 1) * TU + 1)
                for j in range(NT):
                    if m is not None and j == 0:
                        relu(m, NC - 2, NC % 2)
                    if m is not None and j == 3:
                        high(m, NC - 1, (NC - 1) % 2)
                    for n in range(2):
                        act.wait_ge(pe_eq2, (b * NT + j) * 2 + n + 1)
                        nc.scalar.activation(qET[:, 8 * n:8 * n + 8, j * P:(j + 1) * P],
                                             PSH[:, (2, 0)[j % 2] + n, :].rearrange("p (a s) -> p a s", a=8),
                                             ACT.Copy).then_inc(act_eq2, 1)
                    if m is not None and j == 1:
                        relu(m, NC - 1, (NC - 1) % 2)
                        high(m, NC - 2, NC % 2)
                def probabilities(g, gs):
                    for d in range(NU):
                        act.wait_ge(pe_sc, b * TU + g * NU + d + 1)
                        if d == 0:
                            act.wait_ge(pe_pv, b * NG + g + 1)
                        bank = (0, 2, BK_Y)[PAIRS[gs][d]]
                        src = PS[:, bank:bank + 2, :].rearrange("p a c -> p (a c)")
                        if d < HG:
                            dst = PT[gs % 2][:, d, 0:1024]
                        else:
                            dst = PT[gs % 2][:, :, 1024:SW]
                            src = src.rearrange("p (h c) -> p h c", h=HG)
                        nc.scalar.activation(dst, src, ACT.Exp, scale=SCALE).then_inc(act_p, 1)

                probabilities(0, 0)
                probabilities(1, 1)
                with act.Fori(0, NG // 2 - 1) as i:
                    for u in range(2):
                        probabilities(i * 2 + 2 + u, 2 + u)
                for k in range(KT):
                    act.wait_ge(pe_aT, b * KT + k + 1)
                    nc.scalar.activation(aT[:, k, :], PS[:, 4 + k, :], ACT.Copy).then_inc(act_aT, 1)
                if more:
                    stack_high(b + 1, 0, 2)
                    copy_v(b + 1)

            copy_v(0)
            high_w2(0)
            act.wait_ge(dve_w, 2)
            stack_high(0, 0, 2)
            high_w2(1)
            act.wait_ge(s_small, 16 * N_SMALL)
            nc.scalar.activation(CENT[:, 0], CENTF[:, :, :], ACT.Copy).then_inc(act_w, 1)
            nc.scalar.activation(B2[:, 0, :], B2F, ACT.Copy).then_inc(act_w, 1)
            turn(0, None, True)
            with act.Fori(1, B - 1) as b:
                turn(b, b - 1, True)
            turn(B - 1, B - 2, False)
            m = B - 1
            x1T_parts(m)
            route(m)
            chunks(m, 0, 2)
            gate_rows(m)
            chunks(m, 2, NSH)
            for c in range(NSH, NC):
                relu(m, c, c % 2)

        @block.gpsimd
        def _(pool):
            for credit in (pool_v, pool_e):
                pool.sem_inc(credit, 1)
            pool.sem_inc(pool_hp, 2)
            zero = pool.to_reg(0.0)
            whole = lambda t: t[:, :, :].rearrange("p a s -> p (a s)").bitcast(F32)
            nc.gpsimd.memset(whole(kz[1]), 0.0).then_inc(s_one, 1)
            nc.gpsimd.memset(hp[:, :, :, :], 0.0)
            nc.gpsimd.memset(vst[:, :, :, :, HD:HD + 1], 1.0).then_inc(s_init, 1)
            pool.drain()
            pool.wait_ge(dve_w, 2)

            def low(m, c, slot):
                w = CHUNKS[c][1] if isinstance(c, int) else P
                pool.wait_ge(s_high, m * NC + c + 1)
                nc.gpsimd.tensor_tensor(hp[0:w, slot, 1, :], hr[0:w, slot, :], hp[0:w, slot, 0, :],
                                        ALU.subtract).then_inc(pool_hp, 1)

            def turn(b, m):
                settled_wait(pool, pe_pv, b * NG + 2)
                nc.gpsimd.memset(EQ[:, :, :, CR:HW].bitcast(F32), 0.0)
                nc.gpsimd.memset(EK[:, :, :, CR + NCH:HW].bitcast(F32), 0.0)
                for j in range(NT):
                    nc.gpsimd.tensor_scalar(EK[:, j, :, CR:CR + NCH], ind[:, j:j + 1, :].to_broadcast([P, H, NCH]),
                                            1.0, 0.0, ALU.mult, ALU.add)
                    for n, (E, c0, hi, lo, step) in enumerate(((EQ, 0, 0, 2, 1), (EK, D, 0, 1, 2))):
                        pool.wait_ge(act_e, (b * NT + j) * 2 + n + 1)
                        src = rot[:, j, c0:c0 + D].rearrange("p (h d) -> p h d", h=H).unsqueeze(2).to_broadcast([P, H, 2, HD])
                        e4 = E[:, j, :, 0:CR].rearrange("p h (s d) -> p h s d", s=SLOTS)
                        ins = nc.gpsimd.tensor_tensor(e4[:, :, lo:lo + step + 1:step, :], src,
                                                      e4[:, :, hi:hi + step + 1:step, :], ALU.subtract)
                    ins.then_inc(pool_e, 1)
                if m is None:
                    pool.drain()
                    pool.wait_ge(dve_w, 4)
                    nc.gpsimd.memset(whole(kz[0])[HW:P], 0.0).then_inc(s_init, 1)
                    pool.drain()
                if m is not None:
                    for c in range(*C_FIRST):
                        low(m, c, c % 2)
                    for (first, last), steps in ((C_TOPK, NG // 2), (C_MAX, MAX_STEPS)):
                        n = (last - first) // steps
                        pool.drain()
                        with pool.Fori(0, steps) as i:
                            for u in range(n):
                                low(m, i * n + first + u, (first + u) % 2)
                    for c in range(*C_BIAS):
                        low(m, c, c % 2)
                def stage(g, gs):
                    settled_wait(pool, pe_pv, b * NG + g + 1)
                    vg = v[:, :, bass.ds(g * HG * HD, HG * HD)].rearrange("p t (h d) -> p t h d", h=HG)
                    ones = vst[:, gs % 2, :, :, HD:HD + 1].to_broadcast([P, NT, HG, HD])
                    nc.gpsimd.tensor_tensor(vst[:, gs % 2, :, :, 0:HD], vg, ones, ALU.mult).then_inc(pool_v, 1)

                def causal(g, gs):
                    for n, t in enumerate(KORDER):
                        if n in (0, 3):
                            settled_wait(pool, act_p, b * TU + g * NU + (HG if n == 0 else NU) + RING)
                        block = PT[gs % 2][:, :, POFF[t]:POFF[t] + P]
                        nc.gpsimd.affine_select(block, block, [[0, HG], [1, P]], ALU.is_ge, zero, base=0,
                                                channel_multiplier=-1).then_inc(pool_p, 1)

                settled_wait(pool, act_v, (b + 1) * 2)
                stage(0, 0)
                with pool.Fori(0, NG // 2 - 1) as i:
                    for u in range(2):
                        causal(i * 2 + u, u)
                        stage(i * 2 + u + 1, u + 1)
                causal(NG - 2, 0)
                stage(NG - 1, 1)
                causal(NG - 1, 1)

            turn(0, None)
            with pool.Fori(1, B - 1) as b:
                turn(b, b - 1)
            turn(B - 1, B - 2)
            for c in range(NC):
                low(B - 1, c, c % 2)

        @block.vector
        def _(dve):
            for credit in (dve_x1, dve_z, dve_o, dve_otok, dve_h):
                dve.sem_inc(credit, 1)
            dve.sem_inc(dve_cm, RING)
            dve.wait_ge(s_const, 16 * N_CONST)
            nc.vector.memset(gmask[:, :, NCH:TOPW], PAD)
            nc.vector.memset(PS[:, BK_PV, :], 0.0)
            nc.vector.memset(gsp[:, :, 2 * NE:GP], 1.0)
            nc.vector.memset(sc[:, :, NE:TOPW], PAD)
            nc.vector.tensor_tensor(rep[:, :, 0:NCH], gm_c[:, 0:1, :].to_broadcast([P, H, NCH]),
                                    sm_c[:, 0:1, :].to_broadcast([P, H, NCH]), ALU.max)
            dve.drain()
            nc.vector.tensor_scalar(cbias[:, 0], rep[:, :, 0:NCH], -OFF, None, ALU.max).then_inc(s_init, 1)

            def low_w2(n):
                c0, c1 = ((0, 13), (13, NC))[n]
                dve.wait_ge(act_w, n + 3)
                src = qf if n == 0 else kz[0][:, :, :].rearrange("p a s -> p (a s)").bitcast(F32)
                nc.vector.tensor_tensor(W2[:, 1, c0:c1, :].rearrange("p c n -> p (c n)"), src[:, 0:(c1 - c0) * D],
                                        W2[:, 0, c0:c1, :].rearrange("p c n -> p (c n)"), ALU.subtract).then_inc(dve_w, 1)

            def link(ins):
                dve.drain()
                return ins

            def gated(m, c, slot, split=False):
                dve.wait_ge(pe_h, m * NC + c + 1)
                dve.wait_ge(act_h, m * NC + c + 2)
                nc.vector.tensor_tensor(hr[:, slot, :], hr[:, slot, :], PS[:, BK_G, :], ALU.mult).then_inc(dve_h, 1)
                if split:
                    dve.drain()
                    dve.wait_ge(pe_y, m * NC + c + 1)
                    nc.vector.tensor_copy(hp[:, slot, 0, :], hr[:, slot, :]).then_inc(s_high, 1)

            def root_guess(n):
                a, y, t = ms[:, 0:n], ry[:, 0:n], rt[:, 0:n]
                link(nc.vector.tensor_scalar(t.bitcast(I32), a.bitcast(I32), 1, None, ALU.logical_shift_right))
                link(nc.vector.tensor_scalar(y.bitcast(I32), t.bitcast(I32), -1.0, float(ROOT), ALU.mult, ALU.add))

            def newton(n, steps):
                a, y, t = ms[:, 0:n], ry[:, 0:n], rt[:, 0:n]
                for _ in range(steps):
                    link(nc.vector.tensor_tensor(t, y, y, ALU.mult))
                    link(nc.vector.scalar_tensor_tensor(out=t, in0=t, scalar=-0.5, in1=a, op0=ALU.mult, op1=ALU.mult))
                    link(nc.vector.scalar_tensor_tensor(out=y, in0=t, scalar=1.5, in1=y, op0=ALU.add, op1=ALU.mult))

            def layernorm(src, dst, done):
                for j in range(NT):
                    nc.vector.bn_stats(st6[:, j, :], src[:, j, :])
                dve.drain()
                for j in range(NT):
                    nc.vector.bn_aggr(mv[:, j, :], st6[:, j, :])
                dve.drain()
                link(nc.vector.tensor_scalar(ms[:, 0:NT], mv[:, :, 1], 1e-5, None, ALU.add))
                root_guess(NT)
                newton(NT, 3)
                for j in range(NT):
                    nc.vector.tensor_scalar(dst[:, j, :], src[:, j, :], mv[:, j, 0:1], ry[:, j:j + 1],
                                            ALU.subtract, ALU.mult).then_inc(done, 1)

            def x1T_parts(m):
                for k in range(KT):
                    dve.wait_ge(act_x1T, m * KT + k + 1)
                    nc.vector.tensor_tensor(x1T[:, 1, k, :], PS[:, 4 + k, :], x1T[:, 0, k, :], ALU.subtract).then_inc(dve_x1T, 1)

            def route(m, b=None):
                dve.wait_ge(act_rt, m + 1)
                link(nc.vector.tensor_scalar(er[:, :, :], er[:, :, :], 1.0, None, ALU.add))
                link(nc.vector.reciprocal(er[:, :, :], er[:, :, :]))
                link(nc.vector.tensor_tensor(sc[:, :, 0:NE], er[:, :, :], rbias.unsqueeze(1).to_broadcast([P, NT, NE]), ALU.add))
                if b is not None:
                    block_diagonal(b)
                for j in range(NT):
                    nc.vector.max(rtop[:, j, :], sc[:, j, 0:NE])
                dve.drain()
                link(nc.vector.memset(rtop[:, :, KR:8], PAD))
                for j in range(NT):
                    nc.vector.match_replace(rrep[:, j, :], rtop[:, j, :], sc[:, j, :], CHOSEN)
                dve.drain()
                link(nc.vector.scalar_tensor_tensor(out=gat[:, :, :], in0=rrep[:, :, 0:NE], scalar=BIG, in1=sc[:, :, 0:NE],
                                                    op0=ALU.is_gt, op1=ALU.mult))
                link(nc.vector.tensor_reduce(gsum[:, :], gat[:, :, :], AX.X, ALU.add))
                link(nc.vector.tensor_scalar(gsum[:, :], gsum[:, :], 1e-8, None, ALU.max))
                link(nc.vector.reciprocal(gsum[:, :], gsum[:, :]))
                link(nc.vector.tensor_tensor(gat[:, :, :], gat[:, :, :], gsum[:, :].unsqueeze(2).to_broadcast([P, NT, NE]), ALU.mult))
                link(nc.vector.tensor_copy(gsp[:, :, 0:NE], gat[:, :, :]))
                nc.vector.tensor_tensor(gsp[:, :, NE:2 * NE], gat[:, :, :], gsp[:, :, 0:NE], ALU.subtract).then_inc(dve_g, 1)

            def finish(m):
                dve.wait_ge(pe_y, (m + 1) * NC + 2)
                for i in range(2):
                    xs = x1n[:, 2 * i:2 * i + 2, :].rearrange("p t d -> p (t d)")
                    nc.vector.scalar_tensor_tensor(out=xs, in0=xs, scalar=2.0, in1=PS[:, BK_Y + i, :],
                                                   op0=ALU.mult, op1=ALU.add).then_inc(dve_z, 1)
                dve.drain()
                layernorm(x1n, x1n, dve_out)
                dve.drain()

            def rope(b, first, last):
                for j in range(first, last):
                    dve.wait_ge(pe_proj, b * NT + j + 1)
                    t = PS[:, j, :].rearrange("p (h u f) -> p h u f", h=2 * H, u=2)
                    o = rot[:, j, :].rearrange("p (h u f) -> p h u f", h=2 * H, u=2)
                    w = ropeb[:, :].rearrange("p (h u f) -> p h u f", h=2 * H, u=2)
                    cj = cos[:, j:j + 1, :].unsqueeze(2).to_broadcast([P, 2 * H, 2, HD // 2])
                    sj = sin[:, j:j + 1, :].unsqueeze(2).to_broadcast([P, 2 * H, 2, HD // 2])
                    nc.vector.tensor_tensor(w, t, sj, ALU.mult)
                    link(nc.vector.tensor_tensor(o, t, cj, ALU.mult))
                    nc.vector.tensor_tensor(o[:, :, 0, :], o[:, :, 0, :], w[:, :, 1, :], ALU.subtract)
                    nc.vector.tensor_tensor(o[:, :, 1, :], o[:, :, 1, :], w[:, :, 0, :], ALU.add).then_inc(dve_rope, 1)
                    dve.drain()

            def block_diagonal(b):
                dve.wait_ge(pe_km, b + 1 + 1)
                for k in range(KT):
                    nc.vector.tensor_tensor(
                        KB[:, k, :].rearrange("p (h n) -> p h n", n=NCH),
                        PS[:, BK_Y + 1, D + k * NCH:D + (k + 1) * NCH].unsqueeze(1).to_broadcast([P, 16, NCH]),
                        bmask.unsqueeze(2).to_broadcast([P, 16, NCH]), ALU.mult).then_inc(dve_kb, 1)

            def best(b, j, bank):
                dve.wait_ge(pe_gate, b * 3 + j + 1)
                nc.vector.tensor_tensor(gmask[:, :, 0:NCH], PS[:, bank, :].rearrange("p (h n) -> p h n", n=NCH),
                                        gm_c[:, j:j + 1, :].to_broadcast([P, H, NCH]), ALU.add).then_inc(dve_gm, 1)
                dve.drain()
                for h in range(H):
                    nc.vector.max(top8[:, h, :], gmask[:, h, 0:NCH])
                dve.drain()

            def mark():
                link(nc.vector.memset(top8[:, :, TOPK - 1:8], PAD))
                for h in range(H):
                    nc.vector.match_replace(rep[:, h, :], top8[:, h, :], gmask[:, h, :], CHOSEN)

            def select(j):
                dve.drain()
                link(nc.vector.scalar_tensor_tensor(out=cbias[:, j], in0=rep[:, :, 0:NCH], scalar=BIG,
                                                    in1=sm_c[:, j:j + 1, :].to_broadcast([P, H, NCH]),
                                                    op0=ALU.is_le, op1=ALU.mult))

            def turn(b, m, more):
                rope(b, 2, 3)
                if m is not None:
                    x1T_parts(m)
                rope(b, 3, NT)
                if m is not None:
                    route(m, b)
                else:
                    low_w2(0)
                    block_diagonal(b)
                    low_w2(1)
                    dve.wait_ge(act_w, 6)
                    nc.vector.tensor_tensor(CENT[:, 1], CENTF[:, :, :], CENT[:, 0], ALU.subtract).then_inc(dve_w, 1)
                    nc.vector.tensor_tensor(B2[:, 1, :], B2F, B2[:, 0, :], ALU.subtract).then_inc(dve_w, 1)
                    nc.vector.tensor_scalar(WO[:, :, :], WO[:, :, :], onw, None, ALU.mult).then_inc(dve_w, 1)
                waiting = iter(range(*C_TOPK) if m is not None else ())

                def gate_next():
                    for c in waiting:
                        gated(m, c, c % 2, split=True)
                        break

                best(b, 1, 3)
                mark()
                select(1)
                gate_next()
                for j, bank in ((2, 0), (3, 1)):
                    best(b, j, bank)
                    gate_next()
                    mark()
                    gate_next()
                    select(j)
                    gate_next()
                for _ in range(*C_TOPK):
                    gate_next()
                settled_wait(dve, pe_gate, (b + 1) * 3 + 1)
                with dve.Fori(0, MAX_STEPS) as i:
                    for u in range(MU):
                        dve.wait_ge(pe_mx, b * TU + i * MU + u + 1 + 1)
                        h0, d = (i * (NG // MAX_STEPS) + u // NU) * HG, u % NU
                        src = PS[:, 2 * (u % RING):2 * (u % RING) + 2, :].rearrange("p a (c k) -> p (a c) k", k=CHUNK)
                        if d < HG:
                            dst = CM[:, bass.ds(h0 + d, 1), 0:32].rearrange("p o c -> p (o c)")
                        else:
                            dst = CM[:, bass.ds(h0, HG), 32:40]
                            src = src.rearrange("p (h c) k -> p h c k", h=HG)
                        nc.vector.tensor_reduce(dst, src, AX.X, ALU.max).then_inc(dve_cm, 1)
                        for cc, part in dealt(u - 1) if m is not None and u else ():
                            if part == 3:
                                gated(m, i * MC + C_MAX[0] + cc, (C_MAX[0] + cc) % 2)
                dve.drain()
                for j in range(NT):
                    w = CPT * (j + 1)
                    link(nc.vector.scalar_tensor_tensor(out=rep[:, :, 0:w], in0=cbias[:, j, :, 0:w], scalar=UNIT,
                                                        in1=CM[:, :, MOFF[j] // CHUNK:MOFF[j] // CHUNK + w],
                                                        op0=ALU.mult, op1=ALU.add))
                    link(nc.vector.tensor_reduce(negm[:, :], rep[:, :, 0:w], AX.X, ALU.max, negate=True))
                    if j == 0:
                        dve.wait_ge(pe_eq, (b + 1) * NG)
                    nc.vector.scalar_tensor_tensor(out=EQ[:, j, :, CR:CR + NCH],
                                                   in0=negm[:, :].unsqueeze(2).to_broadcast([P, H, NCH]), scalar=1.0 / UNIT,
                                                   in1=cbias[:, j], op0=ALU.mult, op1=ALU.add).then_inc(dve_bias, 1)
                    dve.drain()
                    if m is not None and j >= 2:
                        gated(m, C_BIAS[0] + j - 2, (C_BIAS[0] + j - 2) % 2)
                def sigmoid(i):
                    settled_wait(dve, act_eg, b * 2 + i + 1)
                    e2 = eg[:, 2 * i:2 * i + 2, :].rearrange("p t d -> p (t d)")
                    link(nc.vector.tensor_scalar(e2, e2, 1.0, None, ALU.add))
                    link(nc.vector.reciprocal(e2, e2))

                sigmoid(0)
                if m is not None:
                    finish(m)
                def copy_outputs(g):
                    dve.wait_ge(pe_pv, b * NG + g + 1 + 2)
                    nc.vector.tensor_copy(osb[:, :], PS[:, BK_PV, :]).then_inc(dve_o, 1)

                def keep(g, u):
                    dve.wait_ge(pe_oT, b * NG + g + 1 + 1)
                    nc.vector.tensor_copy(otok[:, :, u * HG:(u + 1) * HG, :],
                                          PS[:, BK_OT, :].rearrange("p (t h d) -> p t h d", t=NT, h=HG)[:, :, :, 0:HD + 1]
                                          ).then_inc(dve_otok, 1)

                def two_groups(i, last):
                    w = 2 * HG * HD
                    eg_i = eg[:, :, bass.ds(i * w, w)]
                    keep(i * 2, 0)
                    copy_outputs(i * 2 + 1)
                    keep(i * 2 + 1, 1)
                    dve.drain()
                    u8, s1 = otok[:, :, :, 0:HD], otok[:, :, :, HD]
                    tok = lambda t: t[:, 0:NT * 2 * HG].rearrange("p (t h) -> p t h", t=NT)
                    nc.vector.tensor_tensor(sq, u8, u8, ALU.mult)
                    link(nc.vector.tensor_tensor(tok(rt), s1, s1, ALU.mult))
                    link(nc.vector.tensor_reduce(tok(ms), sq, AX.X, ALU.add))
                    link(nc.vector.scalar_tensor_tensor(out=tok(ms), in0=tok(rt), scalar=HD * 1e-6, in1=tok(ms),
                                                        op0=ALU.mult, op1=ALU.add))
                    root_guess(NT * 2 * HG)
                    newton(NT * 2 * HG, 1)
                    if not last:
                        copy_outputs(i * 2 + 2)
                    newton(NT * 2 * HG, 2)
                    link(nc.vector.tensor_tensor(sq, u8, tok(ry).unsqueeze(3).to_broadcast([P, NT, 2 * HG, HD]), ALU.mult))
                    eg_4 = eg_i.rearrange("p t (h d) -> p t h d", d=HD)
                    link(nc.vector.scalar_tensor_tensor(out=eg_4, in0=sq, scalar=HD ** 0.5, in1=eg_4,
                                                        op0=ALU.mult, op1=ALU.mult).then_inc(dve_on, 1))

                copy_outputs(0)
                sigmoid(1)
                with dve.Fori(0, NG // 2 - 1) as i:
                    two_groups(i, False)
                two_groups(NG // 2 - 1, True)
                if more:
                    rope(b + 1, 0, 2)
                if m is not None:
                    settled_wait(dve, s_out, 16 * m + 32)
                dve.wait_ge(s_x, 16 * b + 16)
                for i in range(2):
                    dve.wait_ge(pe_att, 2 * b + i + 1)
                    nc.vector.tensor_tensor(x1n[:, 2 * i:2 * i + 2, :].rearrange("p t d -> p (t d)"), PS[:, 4 + i, :],
                                            x[:, 2 * i:2 * i + 2, :].rearrange("p t d -> p (t d)"), ALU.add).then_inc(dve_x1, 1)
                dve.drain()
                layernorm(x1n, x1n, dve_ln)

            rope(0, 0, 2)
            for n in range(2):
                dve.wait_ge(act_w, n + 1)
                nc.vector.tensor_tensor(W1[:, 1, n, :], (UK, UQ)[n][:, 0:FS + FR], W1[:, 0, n, :], ALU.subtract).then_inc(dve_w, 1)
            turn(0, None, True)
            with dve.Fori(1, B - 1) as b:
                turn(b, b - 1, True)
            turn(B - 1, B - 2, False)
            m = B - 1
            x1T_parts(m)
            route(m)
            for c in range(NSH, NC):
                gated(m, c, c % 2, split=True)
            finish(m)


def kernel(**inputs):
    import numpy as np
    import ml_dtypes
    import concourse.bacc as bacc
    from concourse.bass_utils import run_bass_kernel_spmd as run

    a = {k[3:]: np.asarray(val) for k, val in inputs.items()}
    f32 = np.float32
    x = np.ascontiguousarray(a["attn_hidden_states"])
    cf = np.zeros((P, C_W), f32)
    p = np.arange(P)
    cf[:, C_ID:C_ID + P] = np.eye(P, dtype=f32)
    inv_freq = f32(1.0) / np.power(f32(10000.0), np.arange(0, HD, 2, dtype=f32) / f32(HD))
    freqs = np.arange(S, dtype=f32)[:, None] * inv_freq[None, :].astype(f32)
    tab = lambda t: t.astype(f32).reshape(NT, P, HD // 2).transpose(1, 0, 2).reshape(P, -1)
    cf[:, C_COS:C_COS + 16] = tab(np.cos(freqs))
    cf[:, C_SIN:C_SIN + 16] = tab(np.sin(freqs))
    cf[:, C_AVG:C_AVG + CPT] = (p[:, None] // CHUNK == np.arange(CPT)) / f32(CHUNK)
    cf[:, C_BM:C_BM + 16] = p[:, None] // HD == np.arange(16)
    own = (np.arange(NT)[None, :, None] * CPT + p[:, None, None] // CHUNK)
    n = np.arange(NCH)[None, None, :]
    cf[:, C_GM:C_GM + 64] = np.where(n < own, 0.0, -BIG).reshape(P, -1)
    cf[:, C_SM:C_SM + 64] = np.where(n == own, 0.0, -OFF).reshape(P, -1)
    ch = np.zeros((P, H_W), np.float16)
    ch[:, H_ID:H_ID + P] = np.eye(P)
    ch[:, H_IND:H_IND + 64] = np.where(n == own, UNIT, 0.0).reshape(P, -1)
    cg = np.zeros((P, G_W), f32)
    cg[:, G_ID:G_ID + P] = np.eye(P)
    cg[:, G_CQ:G_CQ + P] = np.where(p[None, :] > p[:, None], -BIG, 0.0)
    one = np.zeros((GP, FR), np.float16)
    one[0:2 * NE] = np.tile((np.arange(FR) // DF)[None, :] == np.arange(NE)[:, None], (2, 1))
    cf[:, C_ONW] = np.tile(a["attn_o_norm_weight"], P // HD)
    cf[:, C_RB:C_RB + NE] = a["ffn_bias"][None, :]
    b1 = np.concatenate([a["ffn_shared_b1"].reshape(-1), a["ffn_routed_b1"].reshape(-1)])
    w2f = np.concatenate([a["ffn_shared_w2"].reshape(-1, D), a["ffn_routed_w2"].reshape(-1, D)])
    w2 = np.zeros((NC * P, D), f32)
    for c, (f0, m) in enumerate(CHUNKS):
        cf[0:m, C_B1 + c] = b1[f0:f0 + m]
        w2[c * P:c * P + m] = w2f[f0:f0 + m]
    cols = lambda w: w.transpose(1, 0, 2).reshape(D, -1)
    arrays = {
        "in_xT": x.transpose(0, 2, 1),
        "in_x": x,
        "in_wa": np.concatenate([a["attn_Wq"].T, a["attn_Wk"].T, a["attn_Wv"].T, a["attn_Wg1"].T], axis=1),
        "in_wg2": a["attn_Wg2"].T,
        "in_wo": a["attn_Wo"].T,
        "in_w1": np.concatenate([cols(a["ffn_shared_w1"]), cols(a["ffn_routed_w1"])], axis=1),
        "in_w2": w2,
        "in_cent": a["ffn_centroids"].T,
        "in_b2": np.concatenate([a["ffn_routed_b2"], a["ffn_routed_b2"], a["ffn_shared_b2"]]),
        "in_cf": cf,
        "in_ch": ch,
        "in_cg": cg.astype(ml_dtypes.bfloat16),
        "in_one": one,
    }
    arrays = {key: np.ascontiguousarray(val) for key, val in arrays.items()}
    nc = bacc.Bacc("TRN2", target_bir_lowering=False, num_devices=1)
    args = [nc.dram_tensor(key, val.shape, mybir.dt.from_np(val.dtype), kind="ExternalInput").ap()
            for key, val in arrays.items()]
    args.append(nc.dram_tensor("out", (B, S, D), F32, kind="ExternalOutput").ap())
    build(nc, *args)
    return run(nc, [arrays], core_ids=[0]).results[0]["out"]
```
